# Optimizing a Trainium2 kernel written in Bass

```python
import numpy as np
import jax
import jax.numpy as jnp

def _softmax(x, axis=-1):
    return jax.nn.softmax(x, axis=axis)

def _gelu(x):
    return jax.nn.gelu(x, approximate=True)

def _silu(x):
    return jax.nn.silu(x)

def _sigmoid(x):
    return jax.nn.sigmoid(x)

def _layernorm(x, axis=-1, eps=1e-05):
    m = jnp.mean(x, axis=axis, keepdims=True)
    v = jnp.var(x, axis=axis, keepdims=True)
    return (x - m) / jnp.sqrt(v + eps)

def _scatter_add(tgt, idx, src, axis=0):
    return tgt.at[idx].add(src)

def _segment_sum(src, seg, n):
    return jax.ops.segment_sum(src, seg, n)
kernel_name = 'mk_gnn_preln_d2_gnn_r32_ea6f09'

def setup_inputs(seed: int=0):
    np.random.seed(seed)
    _w = jnp.asarray

    def _rec_inputs():
        import jax
        import jax.numpy as jnp
        _gk = jax.random.key(seed)
        x = -0.0005963 + 1.001 * jax.random.normal(jax.random.fold_in(_gk, 1), (128, 768), jnp.float32)
        src = jax.random.randint(jax.random.fold_in(_gk, 2), (2048,), 0, 128, jnp.int32)
        dst = jnp.minimum((128 * jax.random.uniform(jax.random.fold_in(_gk, 3), (2048,)) ** 2.0).astype(jnp.int32), 4095)
        _o = jnp.argsort(dst, stable=True)
        src = src[_o]
        dst = dst[_o]
        edge_attr_256 = 0.000121155 + 1.00018 * jax.random.normal(jax.random.fold_in(_gk, 12), (2048, 256), jnp.float32)
        return (x, src, dst, edge_attr_256)
    x, src, dst, edge_attr_256 = _rec_inputs()

    def _L0_gnn_setup():
        import jax, jax.numpy as jnp
        import numpy as np
        N_NODES = 128
        N_EDGES = 4096
        D = 768
        DE = 256
        L = 3
        H = 8
        DH = D // H
        EPS = 1e-05

        def _layernorm(x, g, b):
            mu = jnp.mean(x, axis=-1, keepdims=True)
            var = jnp.var(x, axis=-1, keepdims=True)
            return (x - mu) * jax.lax.rsqrt(var + EPS) * g + b
        key = jax.random.key(seed)
        ks = jax.random.split(key, 20)
        s = 0.02
        inp = {'node_features': jax.random.normal(ks[0], (N_NODES, D), jnp.float32), 'edge_index': jax.random.randint(ks[1], (2, N_EDGES), 0, N_NODES, jnp.int64 if jax.config.x64_enabled else jnp.int32), 'edge_features': jax.random.normal(ks[2], (N_EDGES, DE), jnp.float32), 'Wn': jax.random.normal(ks[3], (D, D), jnp.float32) * s, 'bn': jnp.zeros((D,), jnp.float32), 'We': jax.random.normal(ks[4], (D, DE), jnp.float32) * s, 'be': jnp.zeros((D,), jnp.float32), 'W1': jax.random.normal(ks[5], (L, D, 2 * D), jnp.float32) * s, 'b1': jnp.zeros((L, D), jnp.float32), 'ln_g': jnp.ones((L, D), jnp.float32), 'ln_b': jnp.zeros((L, D), jnp.float32), 'W2': jax.random.normal(ks[6], (L, D, D), jnp.float32) * s, 'b2': jnp.zeros((L, D), jnp.float32), 'Wqkv': jax.random.normal(ks[7], (3 * D, D), jnp.float32) * s, 'bqkv': jnp.zeros((3 * D,), jnp.float32), 'Wo': jax.random.normal(ks[8], (D, D), jnp.float32) * s, 'bo': jnp.zeros((D,), jnp.float32)}
        return inp
    _L0_gnn_all = _L0_gnn_setup()
    _L0_gnn_in = {k: v for k, v in _L0_gnn_all.items() if k in ('Wn', 'bn', 'We', 'be', 'W1', 'b1', 'ln_g', 'ln_b', 'W2', 'b2', 'Wqkv', 'bqkv', 'Wo', 'bo')}
    del _L0_gnn_all

    def _L1_gnn_setup():
        import jax, jax.numpy as jnp
        import numpy as np
        N = 625
        DEG = 16
        E = N * DEG
        H = 12
        DIN = 64
        DOUT = 64
        NEG_SLOPE = 0.2
        key = jax.random.key(seed)
        k_h, k_src, k_w, k_al, k_ar, k_wr = jax.random.split(key, 6)
        std = 1.414 * np.sqrt(2.0 / (DIN + DOUT))
        h = jax.random.normal(k_h, (N, H * DIN), dtype=jnp.float32)
        src = jax.random.randint(k_src, (E,), 0, N, dtype=jnp.int64)
        dst = jnp.repeat(jnp.arange(N, dtype=jnp.int64), DEG)
        W = jax.random.normal(k_w, (DOUT, DIN), dtype=jnp.float32) * std
        attn_l = jax.random.normal(k_al, (1, H, DOUT), dtype=jnp.float32) * std
        attn_r = jax.random.normal(k_ar, (1, H, DOUT), dtype=jnp.float32) * std
        W_res = jax.random.normal(k_wr, (DOUT, DIN), dtype=jnp.float32) * std
        return {'h': h, 'src': src, 'dst': dst, 'W': W, 'attn_l': attn_l, 'attn_r': attn_r, 'W_res': W_res}
    _L1_gnn_all = _L1_gnn_setup()
    _L1_gnn_in = {k: v for k, v in _L1_gnn_all.items() if k in ('W', 'attn_l', 'attn_r', 'W_res')}
    del _L1_gnn_all
    return {'x': x, 'src': src, 'dst': dst, 'edge_attr_256': edge_attr_256, 'L0_gnn_Wn': _L0_gnn_in['Wn'], 'L0_gnn_bn': _L0_gnn_in['bn'], 'L0_gnn_We': _L0_gnn_in['We'], 'L0_gnn_be': _L0_gnn_in['be'], 'L0_gnn_W1': _L0_gnn_in['W1'], 'L0_gnn_b1': _L0_gnn_in['b1'], 'L0_gnn_ln_g': _L0_gnn_in['ln_g'], 'L0_gnn_ln_b': _L0_gnn_in['ln_b'], 'L0_gnn_W2': _L0_gnn_in['W2'], 'L0_gnn_b2': _L0_gnn_in['b2'], 'L0_gnn_Wqkv': _L0_gnn_in['Wqkv'], 'L0_gnn_bqkv': _L0_gnn_in['bqkv'], 'L0_gnn_Wo': _L0_gnn_in['Wo'], 'L0_gnn_bo': _L0_gnn_in['bo'], 'L1_gnn_W': _L1_gnn_in['W'], 'L1_gnn_attn_l': _L1_gnn_in['attn_l'], 'L1_gnn_attn_r': _L1_gnn_in['attn_r'], 'L1_gnn_W_res': _L1_gnn_in['W_res']}

def reference(x, src, dst, edge_attr_256, L0_gnn_Wn, L0_gnn_bn, L0_gnn_We, L0_gnn_be, L0_gnn_W1, L0_gnn_b1, L0_gnn_ln_g, L0_gnn_ln_b, L0_gnn_W2, L0_gnn_b2, L0_gnn_Wqkv, L0_gnn_bqkv, L0_gnn_Wo, L0_gnn_bo, L1_gnn_W, L1_gnn_attn_l, L1_gnn_attn_r, L1_gnn_W_res):
    import jax
    import jax.numpy as jnp

    def _L0_gnn_ref(node_features, edge_index, edge_features, Wn, bn, We, be, W1, b1, ln_g, ln_b, W2, b2, Wqkv, bqkv, Wo, bo):
        import jax, jax.numpy as jnp
        import numpy as np
        N_NODES = 128
        N_EDGES = 4096
        D = 768
        DE = 256
        L = 3
        H = 8
        DH = D // H
        EPS = 1e-05

        def _layernorm(x, g, b):
            mu = jnp.mean(x, axis=-1, keepdims=True)
            var = jnp.var(x, axis=-1, keepdims=True)
            return (x - mu) * jax.lax.rsqrt(var + EPS) * g + b
        n = node_features.shape[0]
        nodes = node_features @ Wn.T + bn
        edge_proj = edge_features @ We.T + be
        src, dst = (edge_index[0], edge_index[1])
        for l in range(L):
            msgs = nodes[src] + nodes[dst] + edge_proj
            agg = jax.ops.segment_sum(msgs, dst, num_segments=n)
            combined = jnp.concatenate([nodes, agg], axis=-1)
            h = combined @ W1[l].T + b1[l]
            h = _layernorm(h, ln_g[l], ln_b[l])
            h = jax.nn.relu(h)
            h = h @ W2[l].T + b2[l]
            nodes = h + nodes
        qkv = nodes @ Wqkv.T + bqkv
        q, k, v = jnp.split(qkv, 3, axis=-1)
        q = q.reshape(n, H, DH) * DH ** (-0.5)
        k = k.reshape(n, H, DH)
        v = v.reshape(n, H, DH)
        scores = jnp.einsum('nhd,mhd->hnm', q, k)
        probs = jax.nn.softmax(scores, axis=-1)
        attn = jnp.einsum('hnm,mhd->nhd', probs, v).reshape(n, D)
        attended = attn @ Wo.T + bo
        return nodes + attended

    def _L1_gnn_ref(h, src, dst, W, attn_l, attn_r, W_res):
        import jax, jax.numpy as jnp
        import numpy as np
        N = 625
        DEG = 16
        E = N * DEG
        H = 12
        DIN = 64
        DOUT = 64
        NEG_SLOPE = 0.2
        n = h.shape[0]
        hv = h.reshape(n, H, DIN)
        ft = jnp.einsum('nhd,od->nho', hv, W)
        a1 = jnp.sum(ft * attn_l, axis=-1)
        a2 = jnp.sum(ft * attn_r, axis=-1)
        e = jax.nn.leaky_relu(a1[src] + a2[dst], negative_slope=NEG_SLOPE)
        m = jax.ops.segment_max(e, dst, num_segments=n)
        m = jnp.where(jnp.isfinite(m), m, 0.0)
        w = jnp.exp(e - m[dst])
        denom = jax.ops.segment_sum(w, dst, num_segments=n)
        alpha = w / jnp.maximum(denom[dst], 1e-16)
        msg = alpha[:, :, None] * ft[src]
        agg = jax.ops.segment_sum(msg, dst, num_segments=n)
        res = jnp.einsum('nhd,od->nho', hv, W_res)
        out = jax.nn.relu((agg + res).reshape(n, H * DOUT))
        return out
    edge_index = jnp.stack([src, dst])
    h = jnp.maximum(_layernorm(x, axis=-1), 0.0)
    x = x + _L0_gnn_ref(h, edge_index, edge_attr_256, L0_gnn_Wn, L0_gnn_bn, L0_gnn_We, L0_gnn_be, L0_gnn_W1, L0_gnn_b1, L0_gnn_ln_g, L0_gnn_ln_b, L0_gnn_W2, L0_gnn_b2, L0_gnn_Wqkv, L0_gnn_bqkv, L0_gnn_Wo, L0_gnn_bo)
    h = jnp.maximum(_layernorm(x, axis=-1), 0.0)
    x = x + _L1_gnn_ref(h, src, dst, L1_gnn_W, L1_gnn_attn_l, L1_gnn_attn_r, L1_gnn_W_res)
    return x

_drawn_inputs = setup_inputs


def setup_inputs(seed=0):
    import zlib

    import numpy as np

    out = dict(_drawn_inputs(seed))
    spreads = {'L0_gnn_bn': (0.0, 0.1),
     'L0_gnn_be': (0.0, 0.1),
     'L0_gnn_b1': (0.0, 0.434),
     'L0_gnn_ln_g': (1.0, 0.2),
     'L0_gnn_ln_b': (0.0, 0.1),
     'L0_gnn_b2': (0.0, 0.1),
     'L0_gnn_bqkv': (0.0, 0.1),
     'L0_gnn_bo': (0.0, 0.1)}
    factors = {}
    for name, (base, spread) in spreads.items():
        noise = np.random.default_rng([zlib.crc32(name.encode()), seed]).standard_normal(out[name].shape)
        drawn = base * np.exp(spread * noise) if base else spread * noise
        out[name] = jnp.asarray(drawn.astype(out[name].dtype))
    for name, factor in factors.items():
        out[name] = (out[name] * factor).astype(out[name].dtype)
    return out
```

```python
from contextlib import ExitStack

import concourse.bass as bass
from concourse import mybir

ALU = mybir.AluOpType
ACT = mybir.ActivationFunctionType
AX = mybir.AxisListType
F32 = mybir.dt.float32
BF16 = mybir.dt.bfloat16
I32 = mybir.dt.int32

N = 128
D = 768
DE = 256
E = 2048
L = 3
C = D // 128
HC = C // 2
HF = D // 2
ET = E // 128
NH0, DH0 = 8, 96
NH1, DH1 = 12, 64
QG = HF // DH0
ZG = 4
NG = NH1 // ZG
EPS = 1e-5
SCALE = DH0 ** -0.5
SLOPE = 0.2
MASKED = -1e30

GU = 6
SLOTS = 8
U_N = 2 * C
U_1 = 4 * C
U_L = U_1 + U_N
GROUPS = (U_N + L * U_L + 6 * C) // GU
BIAS = {"n": 0, "1": D, "2": D + L * D, "qkv": D + 2 * L * D, "o": 4 * D + 2 * L * D}
BT = 5 * D + 2 * L * D
BR = BT // 128


def build(nc, x, idx, ef, wstream, we, wo, biases, be, ln_cols, gat_w, gat_wt, gat_attn, out):
    ctx = ExitStack()
    with ctx:
        def sb(name, shape, dt=F32):
            return ctx.enter_context(nc.sbuf_tensor(name, shape, dt))

        def sem(name):
            return ctx.enter_context(nc.semaphore(name))

        banks = [ctx.enter_context(nc.psum_tensor(f"bank{i}", [128, 512], F32)) for i in range(8)]

        ring = sb("ring", [128, SLOTS, GU, HF])
        we_sb = sb("we_sb", [128, DE // 128, D])
        wo_slot = GROUPS % SLOTS
        wo_slots = -(-NH0 * D // (GU * HF))
        assert wo_slot + wo_slots <= SLOTS
        wo_sb = ring[0:DH0].rearrange("p s u f -> p (s u f)")[
            :, wo_slot * GU * HF:wo_slot * GU * HF + NH0 * D].rearrange("p (h f) -> p h f", h=NH0)
        shared = sb("shared", [128, ET * DE + ET * 128 + ET * 64 + (ET * 129 + 1) // 2])
        taken = {"early": 0, "late": 0}

        def share(when, shape, dt=F32):
            size = 1
            for s in shape[1:]:
                size *= s
            words = size if dt == F32 else (size + 1) // 2
            flat = shared[0:shape[0], taken[when]:taken[when] + words]
            taken[when] += words
            if dt != F32:
                flat = flat.bitcast(dt)[:, 0:size]
            if len(shape) == 3:
                return flat.rearrange("p (a b) -> p a b", a=shape[1])
            if len(shape) == 4:
                return flat.rearrange("p (a b c) -> p a b c", a=shape[1], b=shape[2])
            return flat

        ef_sb = share("early", [128, ET, DE])
        x_sb = sb("x_sb", [128, D])
        idx_sb = sb("idx_sb", [128, 2, ET], I32)
        idxf = sb("idxf", [128, 2, ET])
        iota = sb("iota", [128, 128])
        ident = sb("ident", [128, 128])
        identb = sb("identb", [128, 128], BF16)
        ones3 = sb("ones3", [3, 128], BF16)
        onesc = sb("onesc", [128, 1], BF16)
        eps = sb("eps", [128, 1])
        oh_dst = share("early", [128, ET, 128])
        oh_dstb = share("early", [128, ET, 128], BF16)
        oh_srcb = share("early", [128, ET, 129], BF16)
        ef_sumT = sb("ef_sumT", [128, DE // 128, 128])
        countT = sb("countT", [128, 128])
        degree = sb("degree", [128, 1])
        diag = sb("diag", [128, 128])
        mixT = sb("mixT", [128, 128])
        mask = sb("mask", [128, 128], BF16)
        degree_row = sb("degree_row", [1, 128])
        be_sb = sb("be_sb", [1, D])
        edgeT = sb("edgeT", [128, C, 128])
        cols = sb("cols", [128, 2, L * C])
        bias_sb = sb("bias_sb", [BR, 128])
        bias_p = sb("bias_p", [BR, 3, 128], BF16)
        bias_r = sb("bias_r", [BR, 2, 128])
        brow = sb("brow", [3, BT], BF16)
        stats = sb("stats", [128, 2, 6])
        mv = sb("mv", [128, 2])
        std = sb("std", [128, 1])
        rstd = sb("rstd", [128, 1])
        xhat = sb("xhat", [128, D])
        hT = sb("hT", [128, C, 128])
        nodes = sb("nodes", [128, D])
        nodesT = sb("nodesT", [128, C, 128])
        aggT = sb("aggT", [128, C, 128])
        qk = share("late", [128, 4, HF])
        v = share("late", [128, 2, HF])
        qT = sb("qT", [DH0, 2, QG, 128])
        kT = sb("kT", [DH0, 2, QG, 128])
        top = sb("top", [128, 2, QG])
        ntop = sb("ntop", [128, 2, QG])
        probs = share("late", [128, 2, QG, 128])
        psum_ = sb("psum_", [128, 2, QG])
        prec = sb("prec", [128, 2, QG])
        probsT = share("late", [128, 2, QG, 128])
        attnT = sb("attnT", [DH0, NH0, 128])
        xn = sb("xn", [128, D])
        x1 = sb("x1", [128, D])
        w2x = sb("w2x", [DH1, 128])
        attn_lr = sb("attn_lr", [DH1, 2 * NH1])
        wbd = sb("wbd", [128, 2, 128])
        vlr = sb("vlr", [128, C * 2 * NH1])
        a_parts = sb("a_parts", [96, 128], BF16)
        a_mid = sb("a_mid", [2 * NH1, 128], BF16)
        a_rest = sb("a_rest", [2 * NH1, 128])
        sel_l = sb("sel_l", [96, NH1, 128], BF16)
        sel_r = sb("sel_r", [96, NH1, 128], BF16)
        ft = sb("ft", [128, NH1, DH1 + 1])
        res = sb("res", [128, NH1, DH1])
        zl = share("late", [128, NH1, 128])
        nzm = sb("nzm", [128, NH1])
        w = share("late", [128, NH1, 128])
        wT = sb("wT", [128, NH1, 128])
        den = sb("den", [128, NH1])
        rden = sb("rden", [128, NH1])
        agg1 = sb("agg1", [128, NH1, DH1])
        y = sb("y", [128, D])

        in_x, in_idx, in_we, in_wo, in_small, in_bias, in_brow, in_gat, in_wbd = map(
            sem, ["in_x", "in_idx", "in_we", "in_wo", "in_small", "in_bias", "in_brow", "in_gat", "in_wbd"])
        in_ef = [sem(f"in_ef{i}") for i in range(4)]
        in_slot = [sem(f"in_slot{i}") for i in range(SLOTS)]
        own_used = sem("own_used")
        pool_c = sem("pool_c")
        consts = sem("consts")
        sels = sem("sels")
        vchain, achain = sem("vchain"), sem("achain")
        onehot_f, onehot_b = sem("onehot_f"), sem("onehot_b")
        bias_split = sem("bias_split")
        ef_psum, count_psum, vlr_psum = sem("ef_psum"), sem("count_psum"), sem("vlr_psum")
        ef_ready, count_ready, vlr_ready = sem("ef_ready"), sem("count_ready"), sem("vlr_ready")
        wbd_zero = sem("wbd_zero")
        edge_psum, edge_ready = sem("edge_psum"), sem("edge_ready")
        stats_ready, std_ready, xhat_ready = sem("stats_ready"), sem("std_ready"), sem("xhat_ready")
        xhatT_psum, hT_ready = sem("xhatT_psum"), sem("hT_ready")
        nodes_psum, nodes_ready = sem("nodes_psum"), sem("nodes_ready")
        nodesT_psum, nodesT_ready = sem("nodesT_psum"), sem("nodesT_ready")
        agg_psum, agg_ready = sem("agg_psum"), sem("agg_ready")
        h1_psum = sem("h1_psum")
        qkv_psum, qkv_ready = sem("qkv_psum"), sem("qkv_ready")
        qkT_psum, qkT_ready = sem("qkT_psum"), sem("qkT_ready")
        score_psum, top_ready, exp_ready = sem("score_psum"), sem("top_ready"), sem("exp_ready")
        probs_ready, probsT_psum, probsT_ready = sem("probs_ready"), sem("probsT_psum"), sem("probsT_ready")
        attn_psum, attn_ready = sem("attn_psum"), sem("attn_ready")
        o_psum = sem("o_psum")
        a_psum, a_ready = sem("a_psum"), sem("a_ready")
        ft_psum, ft_ready, res_ready = sem("ft_psum"), sem("ft_ready"), sem("res_ready")
        z_psum, zl_ready, nzm_ready, w_ready = sem("z_psum"), sem("zl_ready"), sem("nzm_ready"), sem("w_ready")
        wT_psum, wT_ready = sem("wT_psum"), sem("wT_ready")
        gagg_psum, y_ready, stored = sem("gagg_psum"), sem("y_ready"), sem("stored")

        def unit(u):
            return ring[:, u // GU % SLOTS, u % GU, :]

        assert GU == C
        last_use = [(nodes_psum, 1), (nodes_psum, 2)]
        for l in range(L):
            for half in range(2):
                last_use += [(own_used, 2 * l + half + 1), (h1_psum, 2 * l + half + 1)]
            last_use += [(nodes_psum, 2 * l + 3), (nodes_psum, 2 * l + 4)]
        last_use += [(qkv_psum, i + 1) for i in range(6)]

        def bank3(b, n):
            return banks[b][:, 0:n * 128].rearrange("p (c n) -> p c n", c=n)

        block = ctx.enter_context(nc.Block())

        @block.sync
        def _(sp):
            sp.dma_start(idx_sb[:], idx).then_inc(in_idx, 16)
            for i in range(4):
                sp.dma_start(ef_sb[:, 4 * i:4 * i + 4, :], ef[:, 4 * i:4 * i + 4, :]).then_inc(in_ef[i], 16)
                if i == 0:
                    sp.dma_start(x_sb[:], x).then_inc(in_x, 16)
            for g in range(GROUPS):
                if g >= SLOTS:
                    sp.wait_ge(*last_use[g - SLOTS])
                sp.dma_start(ring[:, g % SLOTS, :, :], wstream[g]).then_inc(in_slot[g % SLOTS], 16)
                if g == U_N // GU - 1:
                    sp.dma_start(we_sb[:], we).then_inc(in_we, 16)
            sp.wait_ge(*last_use[GROUPS - SLOTS + wo_slots - 1])
            sp.dma_start(wo_sb[:], wo).then_inc(in_wo, 16)
            for g in range(NG):
                sp.wait_ge(y_ready, g + 1)
                cs = slice(g * ZG * DH1, (g + 1) * ZG * DH1)
                sp.dma_start(out[:, cs], y[:, cs]).then_inc(stored, 16)
            sp.wait_ge(stored, 16 * NG)

        @block.gpsimd
        def _(pool):
            nc.gpsimd.iota(iota[:], [[1, 128]], base=0, channel_multiplier=0,
                           allow_small_or_imprecise_dtypes=True).then_inc(consts, 1)
            nc.gpsimd.memset(ident[:], 0.0).then_inc(pool_c, 1)
            nc.gpsimd.memset(oh_srcb[:, :, 128:129], 1.0).then_inc(consts, 1)
            nc.gpsimd.memset(ones3[:], 1.0).then_inc(consts, 1)
            nc.gpsimd.memset(onesc[:], 1.0).then_inc(consts, 1)
            nc.gpsimd.memset(eps[:], EPS).then_inc(consts, 1)
            pool.wait_ge(pool_c, 1)
            nc.gpsimd.affine_select(out=ident[:], in_=ident[:], compare_op=ALU.not_equal, fill=1.0, base=0,
                                    pattern=[[-1, 128]], channel_multiplier=1).then_inc(consts, 1)
            nc.gpsimd.memset(wbd[:], 0.0).then_inc(wbd_zero, 1)
            nc.gpsimd.memset(vlr[:], 0.0).then_inc(wbd_zero, 1)
            pool.wait_ge(consts, 6)
            nc.gpsimd.tensor_copy(identb[:], ident[:]).then_inc(sels, 1)
            nc.gpsimd.memset(sel_l[:], 0.0).then_inc(pool_c, 1)
            nc.gpsimd.memset(sel_r[:], 0.0).then_inc(pool_c, 1)
            nc.gpsimd.memset(a_parts[:], 0.0).then_inc(sels, 1)
            nc.gpsimd.memset(ft[:, :, DH1:DH1 + 1], 1.0).then_inc(sels, 1)
            n = 3
            for part in range(3):
                for t, off in ((sel_l, 0), (sel_r, NH1)):
                    pool.wait_ge(pool_c, n)
                    nc.gpsimd.affine_select(out=t[:], in_=t[:], compare_op=ALU.not_equal, fill=1.0,
                                            base=-32 * part - off, pattern=[[-1, NH1], [0, 128]],
                                            channel_multiplier=1).then_inc(pool_c, 1)
                    n += 1
            pool.wait_ge(pool_c, n)
            nc.gpsimd.memset(den[:], 0.0).then_inc(sels, 1)

        @block.tensor
        def _(pe):
            def weights(u):
                if u % GU == 0:
                    g = u // GU
                    pe.wait_ge(in_slot[g % SLOTS], 16 * (g // SLOTS + 1))

            def bias(bank, at, stop=False):
                pe.matmul(bank[:, 0:HF], ones3[:], brow[:, at:at + HF], start=True, stop=stop)

            pe.wait_ge(consts, 6)
            for j in range(ET):
                if j % 4 == 0:
                    pe.wait_ge(onehot_f, j // 4 + 1)
                    pe.wait_ge(in_ef[j // 4], 16)
                for k in range(2):
                    mm = pe.matmul(banks[k][:, 0:128], ef_sb[:, j, k * 128:(k + 1) * 128], oh_dst[:, j, :],
                                   start=j == 0, stop=j == ET - 1)
            mm.then_inc(ef_psum, 1)
            pe.wait_ge(onehot_b, 2)
            for j in range(ET):
                pe.matmul(banks[6][:, 0:128], oh_srcb[:, j, 0:128], oh_dstb[:, j, :], start=j == 0, stop=j == ET - 1)
            for j in range(ET):
                pe.matmul(banks[7][:, 0:129], oh_dstb[:, j, :], oh_srcb[:, j, :], start=j == 0, stop=j == ET - 1)
            for j in range(ET):
                mm = pe.matmul(banks[2][0:1, 0:128], onesc[:], oh_dstb[:, j, :], start=j == 0, stop=j == ET - 1)
            mm.then_inc(count_psum, 1)
            pe.wait_ge(in_gat, 48)
            pe.matmul(banks[3][:, 0:2 * NH1], w2x[:], attn_lr[:], start=True, stop=True).then_inc(vlr_psum, 1)

            def xhat_turn(n):
                for c in range(C):
                    if c % HC == 0:
                        pe.wait_ge(xhat_ready, 2 * n + c // HC + 1)
                    mm = pe.transpose(banks[4 + c // HC][:, c % HC * 128:(c % HC + 1) * 128],
                                      xhat[:, c * 128:(c + 1) * 128], ident[:])
                    if c % HC == HC - 1:
                        mm.then_inc(xhatT_psum, 1)

            def nodes_turn(ver, half):
                pe.wait_ge(nodes_ready, 2 * ver + half + 1)
                for c in range(half * HC, (half + 1) * HC):
                    mm = pe.transpose(banks[4 + half][:, c % HC * 128:(c % HC + 1) * 128],
                                      nodes[:, c * 128:(c + 1) * 128], ident[:])
                mm.then_inc(nodesT_psum, 1)

            def nodes_product(ver, u0, at):
                for half in range(2):
                    if ver == 0:
                        pe.wait_ge(count_ready, 4)
                        pe.wait_ge(vlr_ready, 4)
                    bank = banks[2 + half]
                    bias(bank, at + half * HF)
                    for k in range(C):
                        u = u0 + half * C + k
                        weights(u)
                        pe.wait_ge(hT_ready, C * ver + k + 1)
                        if half == 1 and k == HC:
                            nodes_turn(ver, 0)
                        mm = pe.matmul(bank[:, 0:HF], hT[:, k, :], unit(u), start=False, stop=k == C - 1)
                    mm.then_inc(nodes_psum, 1)

            xhat_turn(0)
            pe.wait_ge(in_brow, 48)
            nodes_product(0, 0, BIAS["n"])

            pe.wait_ge(in_we, 16)
            pe.wait_ge(in_small, 32)
            pe.wait_ge(ef_ready, 1)
            for c in range(C):
                o = banks[6 + c // HC][:, c % HC * 128:(c % HC + 1) * 128]
                cs = slice(c * 128, (c + 1) * 128)
                pe.matmul(o, we_sb[:, 0, cs], ef_sumT[:, 0, :], start=True, stop=False)
                pe.matmul(o, we_sb[:, 1, cs], ef_sumT[:, 1, :], start=False, stop=False)
                mm = pe.matmul(o, be_sb[:, cs], degree_row[:], start=False, stop=True)
            mm.then_inc(edge_psum, 1)

            for l in range(L):
                u0 = U_N + l * U_L

                def aggregate(half):
                    if l == 0:
                        pe.wait_ge(edge_ready, 1)
                    else:
                        pe.wait_ge(agg_ready, 2 * l)
                    for c in range(half * HC, (half + 1) * HC):
                        mm = pe.matmul(banks[6 + half][:, c % HC * 128:(c % HC + 1) * 128],
                                       nodes[:, c * 128:(c + 1) * 128], mixT[:], start=True, stop=True)
                    mm.then_inc(agg_psum, 1)

                aggregate(0)
                for half in range(2):
                    bank = banks[half]
                    bias(bank, BIAS["1"] + l * D + half * HF)
                    for k in range(2 * C):
                        u = u0 + half * 2 * C + k
                        weights(u)
                        if half == 0 and k == 0:
                            pe.wait_ge(nodesT_ready, 2 * l + 1)
                        if half == 0 and k == HC:
                            nodes_turn(l, 1)
                            aggregate(1)
                            pe.wait_ge(nodesT_ready, 2 * l + 2)
                        if half == 0 and k == C:
                            pe.wait_ge(agg_ready, 2 * l + 2)
                        lhs = nodesT[:, k, :] if k < C else aggT[:, k - C, :]
                        mm = pe.matmul(bank[:, 0:HF], lhs, unit(u), start=False, stop=k == 2 * C - 1)
                        if k == C - 1:
                            mm.then_inc(own_used, 1)
                    mm.then_inc(h1_psum, 1)
                xhat_turn(1 + l)
                nodes_product(1 + l, u0 + U_1, BIAS["2"] + l * D)

            u0 = U_N + L * U_L

            def project(i, bank, at):
                if i >= 4:
                    pe.wait_ge(qkv_ready, i - 3)
                bias(bank, BIAS["qkv"] + at)
                for k in range(C):
                    u = u0 + i * C + k
                    weights(u)
                    if i == 0 and k == 0:
                        pe.wait_ge(nodesT_ready, 2 * L + 1)
                    if i == 0 and k == HC:
                        nodes_turn(L, 1)
                        pe.wait_ge(nodesT_ready, 2 * L + 2)
                    mm = pe.matmul(bank[:, 0:HF], nodesT[:, k, :], unit(u), start=False, stop=k == C - 1)
                mm.then_inc(qkv_psum, 1)

            def turn_qk(i):
                pe.wait_ge(qkv_ready, i + 1)
                if i >= 2:
                    pe.wait_ge(qkT_ready, i - 1)
                for h in range(QG):
                    mm = pe.transpose(banks[4 + i % 2][0:DH0, h * 128:(h + 1) * 128],
                                      qk[:, i, h * DH0:(h + 1) * DH0], ident[:])
                mm.then_inc(qkT_psum, 1)

            def scores(g):
                pe.wait_ge(qkT_ready, 2 * g + 2)
                for h in range(QG):
                    mm = pe.matmul(banks[6 + g][:, h * 128:(h + 1) * 128], qT[:, g, h, :], kT[:, g, h, :],
                                   start=True, stop=True)
                mm.then_inc(score_psum, 1)

            def turn_probs(g):
                pe.wait_ge(probs_ready, g + 1)
                pe.wait_ge(qkT_ready, 4)
                for h in range(QG):
                    mm = pe.transpose(banks[4 + g][:, h * 128:(h + 1) * 128], probs[:, g, h, :], ident[:])
                mm.then_inc(probsT_psum, 1)

            def attend(g):
                pe.wait_ge(probsT_ready, g + 1)
                pe.wait_ge(qkv_ready, 5 + g)
                for h in range(QG):
                    mm = pe.matmul(banks[2 + g][0:DH0, h * 128:(h + 1) * 128], v[:, g, h * DH0:(h + 1) * DH0],
                                   probsT[:, g, h, :], start=True, stop=True)
                mm.then_inc(attn_psum, 1)

            def project_out(half, g):
                bank = banks[6 + half]
                if g == 0:
                    pe.wait_ge(exp_ready, half + 1)
                    bias(bank, BIAS["o"] + half * HF)
                pe.wait_ge(attn_ready, g + 1)
                for h in range(g * QG, (g + 1) * QG):
                    mm = pe.matmul(bank[:, 0:HF], attnT[:, h, :], wo_sb[:, h, half * HF:(half + 1) * HF],
                                   start=False, stop=h == NH0 - 1)
                if g == 1:
                    mm.then_inc(o_psum, 1)

            project(0, banks[0], 0)
            project(1, banks[1], D)
            turn_qk(0)
            project(2, banks[2], HF)
            turn_qk(1)
            project(3, banks[3], D + HF)
            scores(0)
            turn_qk(2)
            project(4, banks[0], 2 * D)
            turn_qk(3)
            scores(1)
            project(5, banks[1], 2 * D + HF)
            turn_probs(0)
            attend(0)
            pe.wait_ge(in_wo, 16)
            project_out(0, 0)
            turn_probs(1)
            attend(1)
            project_out(0, 1)
            project_out(1, 0)
            project_out(1, 1)

            xhat_turn(1 + L)
            for c in range(C):
                pe.wait_ge(hT_ready, C * (1 + L) + c + 1)
                mm = pe.matmul(banks[0][0:2 * NH1, 0:128], vlr[:, c * 2 * NH1:(c + 1) * 2 * NH1], hT[:, c, :],
                               start=c == 0, stop=c == C - 1)
            mm.then_inc(a_psum, 1)
            pe.wait_ge(in_wbd, 64)
            pe.wait_ge(qkv_ready, 6)
            pe.wait_ge(attn_ready, 2)
            for c in range(C):
                o = banks[1 + c // 2][:, c % 2 * 256:c % 2 * 256 + 256]
                mm = pe.matmul(o, hT[:, c, :], wbd[:], start=True, stop=True)
                if c % 2 == 1:
                    mm.then_inc(ft_psum, 1)

            pe.wait_ge(sels, 4)
            pe.wait_ge(a_ready, 1)
            zb = [6, 7, 0]
            for g in range(NG):
                bank = banks[zb[g]]
                hs = slice(g * ZG, (g + 1) * ZG)
                pe.matmul(bank3(zb[g], ZG), identb[:], mask[:].unsqueeze(1).to_broadcast([128, ZG, 128]),
                          start=True, stop=False)
                pe.matmul(bank3(zb[g], ZG), a_parts[:], sel_r[:, hs, :], start=False, stop=False)
                for h in range(ZG):
                    mm = pe.matmul(bank[:, h * 128:(h + 1) * 128], sel_l[:, g * ZG + h, :], a_parts[:],
                                   start=False, stop=h == ZG - 1)
                mm.then_inc(z_psum, 1)
            tb = [4, 5, 6]
            for g in range(NG):
                pe.wait_ge(w_ready, ZG * (g + 1))
                for h in range(ZG):
                    mm = pe.transpose(banks[tb[g]][:, h * 128:(h + 1) * 128], w[:, g * ZG + h, :], ident[:])
                mm.then_inc(wT_psum, 1)
                pe.wait_ge(wT_ready, g + 1)
                pe.wait_ge(ft_ready, NG)
                pe.wait_ge(res_ready, NG)
                for h in range(ZG):
                    hh = g * ZG + h
                    mm = pe.matmul(banks[1 + g][:, h * (DH1 + 1):(h + 1) * (DH1 + 1)], wT[:, hh, :], ft[:, hh, :],
                                   start=True, stop=True)
                mm.then_inc(gagg_psum, 1)

        @block.scalar
        def _(act):
            act.dma_start(bias_sb[:], biases).then_inc(in_bias, 16)
            act.dma_start(cols[:], ln_cols).then_inc(in_small, 16)
            act.dma_start(be_sb[:], be).then_inc(in_small, 16)
            act.dma_start(w2x[:, 0:DH1], gat_w).then_inc(in_gat, 16)
            act.dma_start(w2x[:, DH1:128], gat_w).then_inc(in_gat, 16)
            act.dma_start(attn_lr[:], gat_attn).then_inc(in_gat, 16)
            act.wait_ge(bias_split, 3)
            for p in range(3):
                act.dma_start(brow[p:p + 1, :].rearrange("o (r n) -> o r n", n=128),
                              bias_p[:, p, :]).then_inc(in_brow, 16)
            act.wait_ge(wbd_zero, 1)
            for half in range(2):
                for t in range(2):
                    rs = slice(half * DH1, (half + 1) * DH1)
                    act.dma_start(wbd[rs, t, rs], gat_wt[t]).then_inc(in_wbd, 16)

            def std_of(n):
                act.wait_ge(stats_ready, n + 1)
                nc.scalar.activation(std[:], mv[:, 1:2], ACT.Sqrt, bias=eps[:]).then_inc(std_ready, 1)

            def turned_relu(n, l=None):
                for c in range(C):
                    if c % HC == 0:
                        act.wait_ge(xhatT_psum, 2 * n + c // HC + 1)
                    src = banks[4 + c // HC][:, c % HC * 128:(c % HC + 1) * 128]
                    if l is None:
                        nc.scalar.activation(hT[:, c, :], src, ACT.Relu).then_inc(hT_ready, 1)
                    else:
                        i = l * C + c
                        nc.scalar.activation(hT[:, c, :], src, ACT.Relu, scale=cols[:, 0, i:i + 1],
                                             bias=cols[:, 1, i:i + 1]).then_inc(hT_ready, 1)

            def nodesT_out(ver, half):
                act.wait_ge(nodesT_psum, 2 * ver + half + 1)
                nc.scalar.copy(nodesT[:, half * HC:(half + 1) * HC, :], bank3(4 + half, HC)).then_inc(nodesT_ready, 1)

            act.wait_ge(consts, 6)
            std_of(0)
            turned_relu(0)
            act.wait_ge(ef_psum, 1)
            for k in range(2):
                ins = nc.scalar.copy(ef_sumT[:, k, :], banks[k][:, 0:128])
            ins.then_inc(ef_ready, 1)
            nodesT_out(0, 0)
            act.wait_ge(edge_psum, 1)
            for half in range(2):
                ins = nc.scalar.copy(edgeT[:, half * HC:(half + 1) * HC, :], bank3(6 + half, HC))
            ins.then_inc(edge_ready, 1)
            act.wait_ge(in_small, 32)
            for l in range(L):
                nodesT_out(l, 1)
                std_of(1 + l)
                turned_relu(1 + l, l)
                nodesT_out(1 + l, 0)
            nodesT_out(L, 1)

            def qkv_out(i, dst):
                act.wait_ge(qkv_psum, i + 1)
                nc.scalar.copy(dst, banks[[0, 1, 2, 3, 0, 1][i]][:, 0:HF]).then_inc(qkv_ready, 1)

            def exps(g):
                act.wait_ge(top_ready, g + 1)
                for h in range(QG):
                    ins = nc.scalar.activation(probs[:, g, h, :], banks[6 + g][:, h * 128:(h + 1) * 128], ACT.Exp,
                                               bias=ntop[:, g, h:h + 1], scale=SCALE,
                                               accum_out=psum_[:, g, h:h + 1])
                ins.then_inc(exp_ready, 1)

            def probsT_out(g):
                act.wait_ge(probsT_psum, g + 1)
                nc.scalar.copy(probsT[:, g, :, :], bank3(4 + g, QG)).then_inc(probsT_ready, 1)

            for i in range(4):
                qkv_out(i, qk[:, i, :])
            exps(0)
            qkv_out(4, v[:, 0, :])
            exps(1)
            qkv_out(5, v[:, 1, :])
            probsT_out(0)
            probsT_out(1)

            std_of(1 + L)
            turned_relu(1 + L)
            for b in range(NG):
                act.wait_ge(ft_psum, b + 1)
                src = banks[1 + b][:].rearrange("p (c t h o) -> p c t h o", c=2, t=2, h=2)
                nc.scalar.copy(ft[:, 4 * b:4 * b + 4, 0:DH1].rearrange("p (c h) o -> p c h o", c=2),
                               src[:, :, 0, :, :]).then_inc(ft_ready, 1)
                nc.scalar.copy(res[:, 4 * b:4 * b + 4, :].rearrange("p (c h) o -> p c h o", c=2),
                               src[:, :, 1, :, :]).then_inc(res_ready, 1)
            for h in range(NH1):
                if h % ZG == 0:
                    act.wait_ge(nzm_ready, h // ZG + 1)
                nc.scalar.activation(w[:, h, :], zl[:, h, :], ACT.Exp, bias=nzm[:, h:h + 1]).then_inc(w_ready, 1)

        @block.vector
        def _(dve):
            links = [0]

            def link(ins):
                links[0] += 1
                ins.then_inc(vchain, 1)
                dve.wait_ge(vchain, links[0])

            V = nc.vector
            dve.wait_ge(in_idx, 16)
            dve.wait_ge(consts, 6)
            link(V.tensor_copy(idxf[:], idx_sb[:]))
            for j in range(ET):
                ins = V.tensor_scalar(oh_dst[:, j, :], iota[:], idxf[:, 1, j:j + 1], None, ALU.is_equal)
                if j % 4 == 3:
                    ins.then_inc(onehot_f, 1)

            def stats_half(half, src):
                return V.bn_stats(stats[:, half, :], src)

            def aggregate_stats():
                V.bn_aggr(mv[:], stats[:].rearrange("p a b -> p (a b)")).then_inc(stats_ready, 1)

            def normalise(n, halves):
                dve.wait_ge(std_ready, n + 1)
                link(V.reciprocal(rstd[:], std[:]))
                for half in range(2):
                    V.tensor_scalar(xhat[:, half * HF:(half + 1) * HF], halves[half], mv[:, 0:1], rstd[:, 0:1],
                                    ALU.subtract, ALU.mult).then_inc(xhat_ready, 1)

            dve.wait_ge(in_bias, 16)
            link(V.tensor_copy(bias_p[:, 0, :], bias_sb[:]))
            link(V.tensor_tensor(bias_r[:, 0, :], bias_sb[:], bias_p[:, 0, :], ALU.subtract))
            link(V.tensor_copy(bias_p[:, 1, :], bias_r[:, 0, :]))
            V.tensor_tensor(bias_p[:, 2, :], bias_r[:, 0, :], bias_p[:, 1, :], ALU.subtract).then_inc(bias_split, 3)

            dve.wait_ge(in_x, 16)
            link(stats_half(0, x_sb[:, 0:HF]))
            link(stats_half(1, x_sb[:, HF:D]))
            aggregate_stats()
            for j in range(ET):
                V.tensor_scalar(oh_srcb[:, j, 0:128], iota[:], idxf[:, 0, j:j + 1], None, ALU.is_equal)
            normalise(0, [x_sb[:, 0:HF], x_sb[:, HF:D]])
            V.tensor_copy(oh_dstb[:, 0:8, :], oh_dst[:, 0:8, :]).then_inc(onehot_b, 1)
            V.tensor_copy(oh_dstb[:, 8:16, :], oh_dst[:, 8:16, :]).then_inc(onehot_b, 1)

            dve.wait_ge(count_psum, 1)
            V.tensor_copy(countT[:], banks[6][:, 0:128]).then_inc(count_ready, 1)
            link(V.tensor_copy(degree[:], banks[7][:, 128:129]))
            V.tensor_scalar(mask[:], banks[7][:, 0:128], 0.0, MASKED, ALU.is_equal, ALU.mult).then_inc(count_ready, 1)
            V.tensor_copy(degree_row[:], banks[2][0:1, 0:128]).then_inc(count_ready, 1)
            link(V.tensor_scalar(diag[:], ident[:], degree[:, 0:1], None, ALU.mult))
            dve.wait_ge(count_ready, 1)
            V.tensor_tensor(mixT[:], diag[:], countT[:], ALU.add).then_inc(count_ready, 1)
            dve.wait_ge(vlr_psum, 1)
            dve.wait_ge(wbd_zero, 2)
            for half in range(2):
                rs = slice(half * DH1, (half + 1) * DH1)
                for t in range(2):
                    o = half + NH1 * t
                    V.tensor_copy(vlr[rs, o:o + (C - 1) * 26 + 1:26],
                                  banks[3][rs, o:o + 11:2]).then_inc(vlr_ready, 1)

            def nodes_out(ver):
                for half in range(2):
                    hs = slice(half * HF, (half + 1) * HF)
                    dve.wait_ge(nodes_psum, 2 * ver + half + 1)
                    if ver == 0:
                        V.tensor_copy(nodes[:, hs], banks[2 + half][:, 0:HF]).then_inc(nodes_ready, 1)
                    else:
                        V.tensor_tensor(nodes[:, hs], banks[2 + half][:, 0:HF], nodes[:, hs],
                                        ALU.add).then_inc(nodes_ready, 1)

            nodes_out(0)
            dve.wait_ge(edge_ready, 1)
            for l in range(L):
                for half in range(2):
                    dve.wait_ge(agg_psum, 2 * l + half + 1)
                    cs = slice(half * HC, (half + 1) * HC)
                    V.tensor_tensor(aggT[:, cs, :], bank3(6 + half, HC), edgeT[:, cs, :],
                                    ALU.add).then_inc(agg_ready, 1)
                for half in range(2):
                    dve.wait_ge(h1_psum, 2 * l + half + 1)
                    link(stats_half(half, banks[half][:, 0:HF]))
                aggregate_stats()
                normalise(1 + l, [banks[0][:, 0:HF], banks[1][:, 0:HF]])
                nodes_out(1 + l)

            dve.wait_ge(nodes_ready, 2 * (L + 1))
            V.tensor_tensor(xn[:], nodes[:], x_sb[:], ALU.add).then_inc(vchain, 1)
            links[0] += 1

            def qkT_out(i):
                dve.wait_ge(qkT_psum, i + 1)
                V.tensor_copy((qT if i % 2 == 0 else kT)[:, i // 2, :, :],
                              banks[4 + i % 2][0:DH0, :].rearrange("p (h n) -> p h n", h=QG)).then_inc(qkT_ready, 1)

            def tops(g):
                dve.wait_ge(score_psum, g + 1)
                link(V.tensor_reduce(top[:, g, :], bank3(6 + g, QG), AX.X, ALU.max))
                V.tensor_scalar(ntop[:, g, :], top[:, g, :], -SCALE, None, ALU.mult).then_inc(top_ready, 1)

            def divide(g):
                dve.wait_ge(exp_ready, g + 1)
                link(V.reciprocal(prec[:, g, :], psum_[:, g, :]))
                V.tensor_tensor(probs[:, g, :, :], probs[:, g, :, :],
                                prec[:, g, :].unsqueeze(2).to_broadcast([128, QG, 128]), ALU.mult).then_inc(probs_ready, 1)

            def attn_out(g):
                dve.wait_ge(attn_psum, g + 1)
                V.tensor_copy(attnT[:, g * QG:(g + 1) * QG, :],
                              banks[2 + g][0:DH0, :].rearrange("p (h n) -> p h n", h=QG)).then_inc(attn_ready, 1)

            qkT_out(0)
            qkT_out(1)
            tops(0)
            qkT_out(2)
            divide(0)
            qkT_out(3)
            tops(1)
            divide(1)
            attn_out(0)
            attn_out(1)

            for half in range(2):
                hs = slice(half * HF, (half + 1) * HF)
                dve.wait_ge(o_psum, half + 1)
                link(V.tensor_tensor(x1[:, hs], banks[6 + half][:, 0:HF], xn[:, hs], ALU.add))
                link(stats_half(half, x1[:, hs]))
            aggregate_stats()
            normalise(1 + L, [x1[:, 0:HF], x1[:, HF:D]])
            R = 2 * NH1
            dve.wait_ge(a_psum, 1)
            dve.wait_ge(sels, 4)
            a_bank = banks[0][0:R, 0:128]
            link(V.tensor_copy(a_parts[0:R, :], a_bank))
            link(V.tensor_tensor(a_rest[:], a_bank, a_parts[0:R, :], ALU.subtract))
            V.tensor_copy(a_parts[32:32 + R, :], a_rest[:])
            link(V.tensor_copy(a_mid[:], a_rest[:]))
            V.tensor_tensor(a_parts[64:64 + R, :], a_rest[:], a_mid[:], ALU.subtract).then_inc(a_ready, 1)
            zb = [6, 7, 0]
            tb = [4, 5, 6]

            def leaky(g):
                hs = slice(g * ZG, (g + 1) * ZG)
                dve.wait_ge(z_psum, g + 1)
                link(V.tensor_copy(zl[:, hs, :], bank3(zb[g], ZG)))
                link(V.scalar_tensor_tensor(out=zl[:, hs, :], in0=zl[:, hs, :], scalar=SLOPE, in1=zl[:, hs, :],
                                            op0=ALU.mult, op1=ALU.max))
                V.tensor_reduce(nzm[:, hs], zl[:, hs, :], AX.X, ALU.max, negate=True).then_inc(nzm_ready, 1)

            def weigh(g):
                hs = slice(g * ZG, (g + 1) * ZG)
                dve.wait_ge(wT_psum, g + 1)
                V.tensor_tensor(wT[:, hs, :], bank3(tb[g], ZG),
                                countT[:].unsqueeze(1).to_broadcast([128, ZG, 128]), ALU.mult).then_inc(wT_ready, 1)

            def finish(g):
                hs = slice(g * ZG, (g + 1) * ZG)
                dve.wait_ge(gagg_psum, g + 1)
                b = banks[1 + g][:, 0:ZG * (DH1 + 1)].rearrange("p (h o) -> p h o", h=ZG)
                link(V.tensor_scalar(den[:, hs], b[:, :, DH1], 1e-16, None, ALU.max))
                link(V.reciprocal(rden[:, hs], den[:, hs]))
                link(V.tensor_tensor(agg1[:, hs, :], b[:, :, 0:DH1],
                                     rden[:, hs].unsqueeze(2).to_broadcast([128, ZG, DH1]), ALU.mult))
                dve.wait_ge(res_ready, NG)
                link(V.tensor_tensor(agg1[:, hs, :], agg1[:, hs, :], res[:, hs, :], ALU.add))
                cs = slice(g * ZG * DH1, (g + 1) * ZG * DH1)
                V.scalar_tensor_tensor(out=y[:, cs], in0=agg1[:, hs, :].rearrange("p h o -> p (h o)"), scalar=0.0,
                                       in1=x1[:, cs], op0=ALU.max, op1=ALU.add).then_inc(y_ready, 1)

            leaky(0)
            leaky(1)
            weigh(0)
            leaky(2)
            weigh(1)
            finish(0)
            weigh(2)
            finish(1)
            finish(2)


def kernel(**inputs):
    import numpy as np
    import concourse.bacc as bacc
    from concourse.bass_utils import run_bass_kernel_spmd as run

    a = {k: np.asarray(v) for k, v in inputs.items()}

    def units(wt):
        i, o = wt.shape
        return wt.reshape(i // 128, 128, o // HF, HF).transpose(2, 0, 1, 3).reshape(-1, 128, HF)

    pre = "L0_gnn_"
    stream = [units(a[pre + "Wn"].T)]
    for l in range(L):
        stream += [units(a[pre + "W1"][l].T), units(a[pre + "W2"][l].T)]
    wqkv = units(a[pre + "Wqkv"].T).reshape(6, C, 128, HF)
    stream += [wqkv[[0, 2, 1, 3, 4, 5]].reshape(-1, 128, HF)]
    stream = np.concatenate(stream)
    arrays = {
        "x": a["x"],
        "idx": np.stack([a["src"].reshape(128, ET), a["dst"].reshape(128, ET)], 1),
        "ef": a["edge_attr_256"].reshape(128, ET, DE),
        "wstream": stream.reshape(GROUPS, GU, 128, HF).transpose(0, 2, 1, 3),
        "we": a[pre + "We"].T.reshape(DE // 128, 128, D).transpose(1, 0, 2),
        "wo": a[pre + "Wo"].T.reshape(NH0, DH0, D).transpose(1, 0, 2),
        "biases": np.concatenate([a[pre + n].reshape(-1) for n in ("bn", "b1", "b2", "bqkv", "bo")]).reshape(BR, 128),
        "be": a[pre + "be"].reshape(1, D),
        "ln_cols": np.stack([a[pre + n].reshape(L * C, 128).T for n in ("ln_g", "ln_b")], 1),
        "gat_w": a["L1_gnn_W"],
        "gat_wt": np.stack([a["L1_gnn_W"].T, a["L1_gnn_W_res"].T]),
        "gat_attn": np.concatenate([a["L1_gnn_attn_l"][0].T, a["L1_gnn_attn_r"][0].T], 1),
    }
    arrays = {k: np.ascontiguousarray(v) for k, v in arrays.items()}
    nc = bacc.Bacc("TRN2", target_bir_lowering=False, num_devices=1)
    args = [nc.dram_tensor(k, v.shape, mybir.dt.from_np(v.dtype), kind="ExternalInput").ap() for k, v in arrays.items()]
    out = nc.dram_tensor("out", (N, D), F32, kind="ExternalOutput").ap()
    build(nc, *args, out)
    r = run(nc, [arrays], core_ids=[0])
    return r.results[0]["out"]
```

```python
from contextlib import ExitStack

import concourse.bass as bass
from concourse import mybir

ALU = mybir.AluOpType
ACT = mybir.ActivationFunctionType
AX = mybir.AxisListType
F32 = mybir.dt.float32
F32R = mybir.dt.float32r
BF16 = mybir.dt.bfloat16
I32 = mybir.dt.int32

N = 128
D = 768
DE = 256
E = 2048
L = 3
C = D // 128
HC = C // 2
HF = D // 2
ET = E // 128
NH0, DH0 = 8, 96
NH1, DH1 = 12, 64
QG = HF // DH0
ZG = 4
NG = NH1 // ZG
EPS = 1e-5
WARM = 32
SCALE = DH0 ** -0.5
SLOPE = 0.2
MASKED = -1e30

JU = 3
GU = 2 * JU
SLOTS = 8
JSLOTS = 4
G_N = 2
G_1, G_2 = 4, 2
G_L = G_1 + G_2
G_QKV = 6
GROUPS = G_N + L * G_L + G_QKV
J_L = 2 * G_1
JOBS = [(G_N + l * G_L + i // 2, i % 2) for l in range(L) for i in range(J_L)]
JOBS += [(GROUPS - G_QKV + i // 2, i % 2) for i in range(2 * G_QKV)]
BIAS = {"1": (0, 0), "2": (32, 0), "o": (32, L * D), "qkv": (64, 0)}
BW = (L + 1) * D
BT = 4 * D + 2 * L * D
BR = BT // 128

def build(nc, x, idx, ef, wstream, we, wo, biases, small_in, bn, out):
    ctx = ExitStack()
    with ctx:
        def sb(name, shape, dt=F32):
            return ctx.enter_context(nc.sbuf_tensor(name, shape, dt))

        def sem(name):
            return ctx.enter_context(nc.semaphore(name))

        banks = [ctx.enter_context(nc.psum_tensor(f"bank{i}", [128, 512], F32)) for i in range(8)]

        ring = sb("ring", [128, SLOTS, GU, HF])
        we_sb = sb("we_sb", [128, DE // 128, D])
        wo_slot = GROUPS % SLOTS
        wo_slots = -(-NH0 * D // (GU * HF))
        assert wo_slot + wo_slots <= SLOTS
        wo_sb = ring[0:DH0].rearrange("p s u f -> p (s u f)")[
            :, wo_slot * GU * HF:wo_slot * GU * HF + NH0 * D].rearrange("p (h f) -> p h f", h=NH0)
        shared = sb("shared", [128, ET * DE + ET * 128 + ET * 64 + ET * 64])
        taken = {"early": 0, "late": 0}

        def share(when, shape, dt=F32):
            size = 1
            for s in shape[1:]:
                size *= s
            words = size if dt == F32 else (size + 1) // 2
            flat = shared[0:shape[0], taken[when]:taken[when] + words]
            taken[when] += words
            if dt != F32:
                flat = flat.bitcast(dt)[:, 0:size]
            if len(shape) == 3:
                return flat.rearrange("p (a b) -> p a b", a=shape[1])
            if len(shape) == 4:
                return flat.rearrange("p (a b c) -> p a b c", a=shape[1], b=shape[2])
            return flat

        ef_sb = share("early", [128, ET, DE])
        late_at = [(wo_slot + wo_slots) * GU * HF]

        def late(shape):
            size = shape[1] * (shape[2] if len(shape) == 3 else 1)
            flat = ring[0:shape[0]].rearrange("p s u f -> p (s u f)")[:, late_at[0]:late_at[0] + size]
            late_at[0] += size
            assert late_at[0] <= SLOTS * GU * HF
            return flat if len(shape) == 2 else flat.rearrange("p (a b) -> p a b", a=shape[1])

        w_hi = sb("w_hi", [128, JSLOTS, JU, HF], F32R)
        w_lo = sb("w_lo", [128, JSLOTS, JU, HF], F32R)
        x_sb = sb("x_sb", [128, D])
        idx_sb = sb("idx_sb", [128, 2, ET], I32)
        idxf = sb("idxf", [128, 2, ET])
        iota = sb("iota", [128, 128], BF16)
        ident = sb("ident", [128, 128])
        identb = sb("identb", [128, 128], BF16)
        ones = sb("ones", [128, 128], BF16)
        ones_row = sb("ones_row", [1, 128])
        bn_sb = sb("bn_sb", [1, D])
        eps = sb("eps", [128, 1])
        oh_dst = share("early", [128, ET, 128])
        oh_dstb = share("early", [128, ET, 128], BF16)
        oh_srcb = share("early", [128, ET, 128], BF16)
        ef_sumT = sb("ef_sumT", [128, DE // 128, 128])
        countT = sb("countT", [128, 128])
        degree = sb("degree", [128, 128])
        diag = sb("diag", [128, 128])
        mixT = sb("mixT", [128, 128])
        mask = sb("mask", [128, 128], BF16)
        edgeT = sb("edgeT", [128, C, 128])
        SMALL = {"cols": (2 * L + 1) * C, "w2x": 2 * DH1, "attn": 2 * NH1, "wt": 2 * DH1}
        small = sb("small", [128, sum(SMALL.values())])
        at, small_at = 0, {}
        for name, width in SMALL.items():
            small_at[name] = small[:, at:at + width]
            at += width
        cols = small_at["cols"].rearrange("p (a c) -> p a c", c=C)
        w2x = small_at["w2x"][0:DH1]
        attn_lr = small_at["attn"][0:DH1]
        wt2 = small_at["wt"].rearrange("p (t o) -> p t o", t=2)
        bias_sb = sb("bias_sb", [BR, 128])
        bias_p = sb("bias_p", [BR, 3, 128], BF16)
        bias_r = sb("bias_r", [BR, 2, 128])
        brow = sb("brow", [64 + 3, BW], BF16)
        stats = sb("stats", [128, 2, 6])
        mv = sb("mv", [128, 2])
        std = sb("std", [128, 1])
        spare = sb("spare", [128, 1])
        rstd = sb("rstd", [128, 1])
        xhat = sb("xhat", [128, D])
        hT = sb("hT", [128, C, 128])
        nodes = sb("nodes", [128, D])
        nodesT_hi = sb("nodesT_hi", [128, C, 128], F32R)
        nodesT_lo = sb("nodesT_lo", [128, C, 128], F32R)
        agg = xhat[:].rearrange("p (c n) -> p c n", c=C)
        aggT_hi = sb("aggT_hi", [128, C, 128], F32R)
        aggT_lo = sb("aggT_lo", [128, C, 128], F32R)
        qk = share("late", [128, 4, HF])
        v = share("late", [128, 2, HF])
        qT = we_sb[0:DH0].rearrange("p a d -> p (a d)")[:, 0:2 * QG * 128].rearrange(
            "p (g h n) -> p g h n", g=2, h=QG)
        kT = sb("kT", [DH0, 2, QG, 128])
        top = sb("top", [128, 2, QG])
        ntop = sb("ntop", [128, 2, QG])
        probs = share("late", [128, 2, QG, 128])
        psum_ = sb("psum_", [128, 2, QG])
        prec = sb("prec", [128, 2, QG])
        probsT = share("late", [128, 2, QG, 128])
        attnT = late([DH0, NH0, 128])
        xn = share("late", [128, D])
        x1 = late([128, D])
        wbd = sb("wbd", [128, 2, 128])
        vlr = sb("vlr", [128, C * 2 * NH1])
        a_parts = sb("a_parts", [96, 128], BF16)
        a_mid = sb("a_mid", [2 * NH1, 128], BF16)
        a_rest = sb("a_rest", [2 * NH1, 128])
        sel_l = sb("sel_l", [96, NH1, 128], BF16)
        sel_r = sb("sel_r", [96, NH1, 128], BF16)
        ft = late([128, NH1, DH1 + 1])
        res = late([128, NH1, DH1])
        zl = share("late", [128, NH1, 128])
        nzm = sb("nzm", [128, NH1])
        w = share("late", [128, NH1, 128])
        wT = late([128, NH1, 128])
        den = sb("den", [128, NH1])
        rden = sb("rden", [128, NH1])
        agg1 = late([128, NH1, DH1])
        y = late([128, D])

        in_x, in_idx, in_we, in_wo, in_small, in_bias, in_bn = map(
            sem, ["in_x", "in_idx", "in_we", "in_wo", "in_small", "in_bias", "in_bn"])
        in_brow = [sem(f"in_brow{i}") for i in range(3)]
        in_ef = [sem(f"in_ef{i}") for i in range(4)]
        in_slot = [sem(f"in_slot{i}") for i in range(SLOTS)]
        hi_ready, lo_ready, job_used = sem("hi_ready"), sem("lo_ready"), sem("job_used")
        pool_c = sem("pool_c")
        consts, ones_ready, wbd_ready = sem("consts"), sem("ones_ready"), sem("wbd_ready")
        ft_ones = sem("ft_ones")
        sels = sem("sels")
        vchain, achain = sem("vchain"), sem("achain")
        onehot_f, onehot_b = sem("onehot_f"), sem("onehot_b")
        bias_split = sem("bias_split")
        ef_psum, count_psum, vlr_psum = sem("ef_psum"), sem("count_psum"), sem("vlr_psum")
        ef_ready, count_ready, vlr_ready = sem("ef_ready"), sem("count_ready"), sem("vlr_ready")
        wbd_zero = sem("wbd_zero")
        edge_psum, edge_ready = sem("edge_psum"), sem("edge_ready")
        stats_ready, std_ready, xhat_ready = sem("stats_ready"), sem("std_ready"), sem("xhat_ready")
        xhatT_psum, hT_ready = sem("xhatT_psum"), sem("hT_ready")
        nodes_psum, nodes_ready = sem("nodes_psum"), sem("nodes_ready")
        nodesT_psum, nodesT_hi_ready, nodesT_lo_ready = sem("nodesT_psum"), sem("nodesT_hi_ready"), sem("nodesT_lo_ready")
        agg_psum, agg_ready = sem("agg_psum"), sem("agg_ready")
        agg_hi_ready, agg_lo_ready = sem("agg_hi_ready"), sem("agg_lo_ready")
        h1_psum = sem("h1_psum")
        qkv_psum, qkv_ready = sem("qkv_psum"), sem("qkv_ready")
        qkT_psum, qkT_ready = sem("qkT_psum"), sem("qkT_ready")
        score_psum, top_ready, exp_ready = sem("score_psum"), sem("top_ready"), sem("exp_ready")
        probs_ready, probsT_psum, probsT_ready = sem("probs_ready"), sem("probsT_psum"), sem("probsT_ready")
        attn_psum, attn_ready = sem("attn_psum"), sem("attn_ready")
        o_psum = sem("o_psum")
        a_psum, a_ready = sem("a_psum"), sem("a_ready")
        ft_psum, ft_ready, res_ready = sem("ft_psum"), sem("ft_ready"), sem("res_ready")
        z_psum, zl_ready, nzm_ready, w_ready = sem("z_psum"), sem("zl_ready"), sem("nzm_ready"), sem("w_ready")
        wT_psum, wT_ready = sem("wT_psum"), sem("wT_ready")
        gagg_psum, y_ready, stored = sem("gagg_psum"), sem("y_ready"), sem("stored")

        def unit(g, i):
            return ring[:, g % SLOTS, i, :]

        last_use = [(nodes_psum, 1), (nodes_psum, 2)]
        for l in range(L):
            last_use += [(lo_ready, J_L * l + 2 * i + 2) for i in range(G_1)]
            last_use += [(nodes_psum, 2 * l + 3), (nodes_psum, 2 * l + 4)]
        last_use += [(lo_ready, J_L * L + 2 * i + 2) for i in range(G_QKV)]

        def bank3(b, n):
            return banks[b][:, 0:n * 128].rearrange("p (c n) -> p c n", c=n)

        block = ctx.enter_context(nc.Block())

        @block.sync
        def _(sp):
            def load(g):
                if g >= SLOTS:
                    sp.wait_ge(*last_use[g - SLOTS])
                sp.dma_start(ring[:, g % SLOTS, :, :], wstream[g]).then_inc(in_slot[g % SLOTS], 16)

            sp.dma_start(idx_sb[:], idx).then_inc(in_idx, 16)
            for i in range(4):
                sp.dma_start(ef_sb[:, 4 * i:4 * i + 4, :], ef[:, 4 * i:4 * i + 4, :]).then_inc(in_ef[i], 16)
                if i == 0:
                    sp.dma_start(x_sb[:], x).then_inc(in_x, 16)
            for g in range(G_N + 2):
                load(g)
            sp.dma_start(we_sb[:], we).then_inc(in_we, 16)
            for g in range(G_N + 2, GROUPS):
                load(g)
            for i in range(wo_slots):
                sp.wait_ge(*last_use[GROUPS - SLOTS + i])
            sp.dma_start(wo_sb[:], wo).then_inc(in_wo, 16)
            for g in range(NG):
                sp.wait_ge(y_ready, g + 1)
                cs = slice(g * ZG * DH1, (g + 1) * ZG * DH1)
                sp.dma_start(out[:, cs], y[:, cs]).then_inc(stored, 16)
            sp.wait_ge(stored, 16 * NG)

        @block.gpsimd
        def _(pool):
            nc.gpsimd.iota(iota[:], [[1, 128]], base=0, channel_multiplier=0,
                           allow_small_or_imprecise_dtypes=True).then_inc(consts, 1)
            nc.gpsimd.memset(ones[:], 1.0).then_inc(ones_ready, 1)
            nc.gpsimd.memset(ones_row[:], 1.0).then_inc(ones_ready, 1)
            nc.gpsimd.memset(eps[:], EPS).then_inc(consts, 1)
            nc.gpsimd.memset(ident[:], 0.0).then_inc(pool_c, 1)
            pool.wait_ge(pool_c, 1)
            nc.gpsimd.affine_select(out=ident[:], in_=ident[:], compare_op=ALU.not_equal, fill=1.0, base=0,
                                    pattern=[[-1, 128]], channel_multiplier=1).then_inc(consts, 1)
            nc.gpsimd.memset(wbd[:], 0.0).then_inc(wbd_zero, 1)
            nc.gpsimd.memset(vlr[:], 0.0).then_inc(wbd_zero, 1)
            pool.wait_ge(bias_split, 1)
            r = 0
            for i, rows in enumerate((L * C, (L + 1) * C, L * C)):
                for p in range(3):
                    pool.dma_start(brow[32 * i + p:32 * i + p + 1, 0:rows * 128].rearrange("o (r n) -> o r n", n=128),
                                   bias_p[r:r + rows, p, :]).then_inc(in_brow[i], 16)
                r += rows
            pool.wait_ge(consts, 3)
            nc.gpsimd.tensor_copy(identb[:], ident[:]).then_inc(sels, 1)
            pool.wait_ge(in_small, 16)
            pool.wait_ge(wbd_zero, 1)
            pool.wait_ge(sels, 1)
            for half in range(2):
                rs = slice(half * DH1, (half + 1) * DH1)
                if half:
                    pool.wait_ge(wbd_ready, half)
                nc.gpsimd.tensor_copy(wbd[rs, :, rs], wt2[rs, :, :]).then_inc(wbd_ready, 1)
            pool.wait_ge(wbd_ready, 2)
            nc.gpsimd.memset(sel_l[:], 0.0).then_inc(pool_c, 1)
            nc.gpsimd.memset(sel_r[:], 0.0).then_inc(pool_c, 1)
            nc.gpsimd.memset(a_parts[:], 0.0).then_inc(sels, 1)
            n = 3
            for part in range(3):
                for t, off in ((sel_l, 0), (sel_r, NH1)):
                    pool.wait_ge(pool_c, n)
                    nc.gpsimd.affine_select(out=t[:], in_=t[:], compare_op=ALU.not_equal, fill=1.0,
                                            base=-32 * part - off, pattern=[[-1, NH1], [0, 128]],
                                            channel_multiplier=1).then_inc(pool_c, 1)
                    n += 1
            pool.wait_ge(pool_c, n)
            nc.gpsimd.memset(den[:], 0.0).then_inc(sels, 1)
            pool.wait_ge(lo_ready, len(JOBS))
            nc.gpsimd.memset(ft[:, :, DH1:DH1 + 1], 1.0).then_inc(ft_ones, 1)

        @block.tensor
        def _(pe):
            def landed(g):
                pe.wait_ge(in_slot[g % SLOTS], 16 * (g // SLOTS + 1))

            def bias(bank, name, at, stop=False):
                p, c = BIAS[name]
                pe.wait_ge(in_brow[p // 32], 48)
                return pe.matmul(bank[:, 0:HF], ones[p:p + 3, :], brow[p:p + 3, c + at:c + at + HF],
                                 start=False, stop=stop)

            def products(bank, j, his, los, start, act_lo):
                js = j % JSLOTS
                pe.wait_ge(hi_ready, j + 1)
                for i in range(JU):
                    pe.matmul(bank[:, 0:HF], his[i], w_hi[:, js, i, :], start=start and i == 0, stop=False)
                pe.wait_ge(lo_ready, j + 1)
                for i in range(JU):
                    pe.matmul(bank[:, 0:HF], his[i], w_lo[:, js, i, :], start=False, stop=False)
                pe.wait_ge(*act_lo)
                for i in range(JU):
                    mm = pe.matmul(bank[:, 0:HF], los[i], w_hi[:, js, i, :], start=False, stop=False)
                mm.then_inc(job_used, 1)

            pe.wait_ge(ones_ready, 1)
            for _ in range(WARM):
                pe.matmul(banks[5][:, 0:128], ones[:], ones[:], start=True, stop=True)

            for j in range(ET):
                if j % 4 == 0:
                    pe.wait_ge(onehot_f, j // 4 + 1)
                    pe.wait_ge(in_ef[j // 4], 16)
                for k in range(2):
                    mm = pe.matmul(banks[k][:, 0:128], ef_sb[:, j, k * 128:(k + 1) * 128],
                                   oh_dst[:, j, :], start=j == 0, stop=j == ET - 1)
            mm.then_inc(ef_psum, 1)

            def xhat_turn(n):
                for c in range(C):
                    if c % HC == 0:
                        pe.wait_ge(xhat_ready, 2 * n + c // HC + 1)
                    mm = pe.transpose(banks[4 + c // HC][:, c % HC * 128:(c % HC + 1) * 128],
                                      xhat[:, c * 128:(c + 1) * 128], ident[:])
                    if c % HC == HC - 1:
                        mm.then_inc(xhatT_psum, 1)

            def nodes_turn(ver, half):
                pe.wait_ge(nodes_ready, 2 * ver + half + 1)
                for c in range(half * HC, (half + 1) * HC):
                    mm = pe.transpose(banks[4 + half][:, c % HC * 128:(c % HC + 1) * 128],
                                      nodes[:, c * 128:(c + 1) * 128], ident[:])
                mm.then_inc(nodesT_psum, 1)

            def nodes_product(ver, g0):
                for half in range(2):
                    if ver == 0:
                        pe.wait_ge(count_ready, 4)
                        pe.wait_ge(vlr_ready, 4)
                    bank = banks[2 + half]
                    landed(g0 + half)
                    for k in range(C):
                        pe.wait_ge(hT_ready, C * ver + k + 1)
                        if half == 1 and k == HC:
                            nodes_turn(ver, 0)
                        if k == C - 1 and ver > 0:
                            bias(bank, "2", (ver - 1) * D + half * HF)
                        elif k == C - 1:
                            pe.wait_ge(in_bn, 16)
                            pe.wait_ge(ones_ready, 2)
                            pe.matmul(bank[:, 0:HF], ones_row[:], bn_sb[:, half * HF:(half + 1) * HF],
                                      start=False, stop=False)
                        mm = pe.matmul(bank[:, 0:HF], hT[:, k, :], unit(g0 + half, k), start=k == 0, stop=k == C - 1)
                    mm.then_inc(nodes_psum, 1)

            def nodes_job(bank, ver, j, part, start=False):
                if ver == 0 and start:
                    pe.wait_ge(ef_ready, 1)
                ks = range(part * HC, (part + 1) * HC)
                pe.wait_ge(nodesT_hi_ready, 2 * ver + part + 1)
                products(bank, j, [nodesT_hi[:, k, :] for k in ks], [nodesT_lo[:, k, :] for k in ks], start,
                         (nodesT_lo_ready, 2 * ver + part + 1))

            def aggregate(l, half):
                pe.wait_ge(agg_ready, 2 * l)
                for c in range(half * HC, (half + 1) * HC):
                    mm = pe.matmul(banks[6 + half][:, c % HC * 128:(c % HC + 1) * 128],
                                   nodes[:, c * 128:(c + 1) * 128], mixT[:], start=True, stop=True)
                mm.then_inc(agg_psum, 1)

            def agg_job(bank, l, j, part):
                ks = range(part * HC, (part + 1) * HC)
                pe.wait_ge(agg_hi_ready, 2 * l + part + 1)
                products(bank, j, [aggT_hi[:, k, :] for k in ks], [aggT_lo[:, k, :] for k in ks], False,
                         (agg_lo_ready, 2 * l + part + 1))

            pe.wait_ge(consts, 3)
            xhat_turn(0)
            pe.wait_ge(onehot_b, 2)
            for j in range(ET):
                pe.matmul(banks[6][:, 0:128], oh_srcb[:, j, :], oh_dstb[:, j, :], start=j == 0, stop=j == ET - 1)
            for j in range(ET):
                pe.matmul(banks[7][:, 0:128], oh_dstb[:, j, :], oh_srcb[:, j, :], start=j == 0, stop=j == ET - 1)
            for j in range(ET):
                mm = pe.matmul(banks[2][:, 0:128], ones[:], oh_dstb[:, j, :], start=j == 0, stop=j == ET - 1)
            mm.then_inc(count_psum, 1)
            pe.wait_ge(in_small, 16)
            pe.matmul(banks[3][:, 0:2 * NH1], w2x, attn_lr, start=True, stop=True).then_inc(vlr_psum, 1)
            nodes_product(0, 0)

            for l in range(L):
                j0 = J_L * l
                h0, h1 = banks[0], banks[1]
                nodes_job(h0, l, j0, 0, start=True)
                nodes_turn(l, 1)
                if l > 0:
                    aggregate(l, 0)
                    aggregate(l, 1)
                nodes_job(h1, l, j0 + 1, 0, start=True)
                nodes_job(h0, l, j0 + 2, 1)
                nodes_job(h1, l, j0 + 3, 1)
                if l == 0:
                    pe.wait_ge(in_we, 16)
                    pe.wait_ge(ef_ready, 1)
                    for c in range(C):
                        o = banks[6 + c // HC][:, c % HC * 128:(c % HC + 1) * 128]
                        cs = slice(c * 128, (c + 1) * 128)
                        pe.matmul(o, we_sb[:, 0, cs], ef_sumT[:, 0, :], start=True, stop=False)
                        mm = pe.matmul(o, we_sb[:, 1, cs], ef_sumT[:, 1, :], start=False, stop=True)
                    mm.then_inc(edge_psum, 1)
                    pe.wait_ge(edge_ready, 1)
                    aggregate(l, 0)
                    aggregate(l, 1)
                for half in range(2):
                    bank = banks[half]
                    agg_job(bank, l, j0 + 4 + 2 * half, 0)
                    agg_job(bank, l, j0 + 5 + 2 * half, 1)
                    bias(bank, "1", l * D + half * HF, stop=True).then_inc(h1_psum, 1)
                xhat_turn(1 + l)
                nodes_product(1 + l, G_N + l * G_L + G_1)

            j0 = J_L * L
            qkv_banks = [banks[i] for i in (0, 1, 2, 3, 0, 1)]

            def project(i, part, job):
                if i >= 4 and part == 0:
                    pe.wait_ge(qkv_ready, i - 3)
                nodes_job(qkv_banks[i], L, j0 + job, part, start=part == 0)
                if part == 1:
                    at = [0, D, HF, D + HF, 2 * D, 2 * D + HF][i]
                    bias(qkv_banks[i], "qkv", at, stop=True).then_inc(qkv_psum, 1)

            def turn_qk(i):
                pe.wait_ge(qkv_ready, i + 1)
                if i >= 2:
                    pe.wait_ge(qkT_ready, i - 1)
                for h in range(QG):
                    mm = pe.transpose(banks[4 + i % 2][0:DH0, h * 128:(h + 1) * 128],
                                      qk[:, i, h * DH0:(h + 1) * DH0], ident[:])
                mm.then_inc(qkT_psum, 1)

            def scores(g):
                pe.wait_ge(qkT_ready, 2 * g + 2)
                for h in range(QG):
                    mm = pe.matmul(banks[6 + g][:, h * 128:(h + 1) * 128], qT[:, g, h, :], kT[:, g, h, :],
                                   start=True, stop=True)
                mm.then_inc(score_psum, 1)

            def turn_probs(g):
                pe.wait_ge(probs_ready, g + 1)
                pe.wait_ge(qkT_ready, 4)
                for h in range(QG):
                    mm = pe.transpose(banks[4 + g][:, h * 128:(h + 1) * 128], probs[:, g, h, :], ident[:])
                mm.then_inc(probsT_psum, 1)

            def attend(g):
                pe.wait_ge(probsT_ready, g + 1)
                pe.wait_ge(qkv_ready, 5 + g)
                for h in range(QG):
                    mm = pe.matmul(banks[2 + g][0:DH0, h * 128:(h + 1) * 128], v[:, g, h * DH0:(h + 1) * DH0],
                                   probsT[:, g, h, :], start=True, stop=True)
                mm.then_inc(attn_psum, 1)

            def project_out(half, g):
                bank = banks[6 + half]
                if g == 0:
                    pe.wait_ge(exp_ready, half + 1)
                pe.wait_ge(attn_ready, g + 1)
                for h in range(g * QG, (g + 1) * QG):
                    mm = pe.matmul(bank[:, 0:HF], attnT[:, h, :], wo_sb[:, h, half * HF:(half + 1) * HF],
                                   start=h == 0, stop=h == NH0 - 1)
                    if h == 0:
                        bias(bank, "o", half * HF)
                if g == 1:
                    mm.then_inc(o_psum, 1)

            project(0, 0, 0)
            nodes_turn(L, 1)
            project(1, 0, 1)
            project(0, 1, 2)
            project(1, 1, 3)
            project(2, 0, 4)
            turn_qk(0)
            turn_qk(1)
            project(2, 1, 5)
            scores(0)
            project(3, 0, 6)
            project(3, 1, 7)
            project(4, 0, 8)
            turn_qk(2)
            turn_qk(3)
            project(4, 1, 9)
            scores(1)
            turn_probs(0)
            project(5, 0, 10)
            project(5, 1, 11)
            attend(0)
            pe.wait_ge(in_wo, 16)
            project_out(0, 0)
            project_out(1, 0)
            turn_probs(1)
            attend(1)
            project_out(0, 1)
            project_out(1, 1)

            xhat_turn(1 + L)
            for c in range(C):
                pe.wait_ge(hT_ready, C * (1 + L) + c + 1)
                mm = pe.matmul(banks[0][0:2 * NH1, 0:128], vlr[:, c * 2 * NH1:(c + 1) * 2 * NH1], hT[:, c, :],
                               start=c == 0, stop=c == C - 1)
            mm.then_inc(a_psum, 1)
            pe.wait_ge(wbd_ready, 2)
            pe.wait_ge(qkv_ready, 6)
            pe.wait_ge(attn_ready, 2)
            for c in range(C):
                o = banks[1 + c // 2][:, c % 2 * 256:c % 2 * 256 + 256]
                mm = pe.matmul(o, hT[:, c, :], wbd[:], start=True, stop=True)
                if c % 2 == 1:
                    mm.then_inc(ft_psum, 1)

            pe.wait_ge(sels, 3)
            pe.wait_ge(a_ready, 1)
            zb = [6, 7, 0]
            for g in range(NG):
                bank = banks[zb[g]]
                hs = slice(g * ZG, (g + 1) * ZG)
                pe.matmul(bank3(zb[g], ZG), identb[:], mask[:].unsqueeze(1).to_broadcast([128, ZG, 128]),
                          start=True, stop=False)
                pe.matmul(bank3(zb[g], ZG), a_parts[:], sel_r[:, hs, :], start=False, stop=False)
                for h in range(ZG):
                    mm = pe.matmul(bank[:, h * 128:(h + 1) * 128], sel_l[:, g * ZG + h, :], a_parts[:],
                                   start=False, stop=h == ZG - 1)
                mm.then_inc(z_psum, 1)
            tb = [4, 5, 6]

            def turn_weights(g):
                pe.wait_ge(w_ready, ZG * (g + 1))
                for h in range(ZG):
                    mm = pe.transpose(banks[tb[g]][:, h * 128:(h + 1) * 128], w[:, g * ZG + h, :], ident[:])
                mm.then_inc(wT_psum, 1)

            def gather(g):
                pe.wait_ge(wT_ready, g + 1)
                pe.wait_ge(ft_ready, NG)
                pe.wait_ge(ft_ones, 1)
                pe.wait_ge(res_ready, NG)
                for h in range(ZG):
                    hh = g * ZG + h
                    mm = pe.matmul(banks[1 + g][:, h * (DH1 + 1):(h + 1) * (DH1 + 1)], wT[:, hh, :], ft[:, hh, :],
                                   start=True, stop=True)
                mm.then_inc(gagg_psum, 1)

            turn_weights(0)
            turn_weights(1)
            gather(0)
            turn_weights(2)
            gather(1)
            gather(2)

        @block.scalar
        def _(act):
            act.dma_start(bias_sb[:], biases).then_inc(in_bias, 16)
            act.dma_start(bn_sb[:], bn).then_inc(in_bn, 16)
            act.dma_start(small[:], small_in).then_inc(in_small, 16)

            def std_of(n):
                act.wait_ge(stats_ready, n + 1)
                nc.scalar.activation(std[:], mv[:, 1:2], ACT.Sqrt, bias=eps[:]).then_inc(std_ready, 1)

            def turned_relu(n, l=None):
                for c in range(C):
                    if c % HC == 0:
                        act.wait_ge(xhatT_psum, 2 * n + c // HC + 1)
                    src = banks[4 + c // HC][:, c % HC * 128:(c % HC + 1) * 128]
                    if l is None:
                        nc.scalar.activation(hT[:, c, :], src, ACT.Relu).then_inc(hT_ready, 1)
                    else:
                        nc.scalar.activation(hT[:, c, :], src, ACT.Relu, scale=cols[:, l, c:c + 1],
                                             bias=cols[:, L + l, c:c + 1]).then_inc(hT_ready, 1)

            def nodesT_high(ver, half):
                act.wait_ge(nodesT_psum, 2 * ver + half + 1)
                nc.scalar.copy(nodesT_hi[:, half * HC:(half + 1) * HC, :],
                               bank3(4 + half, HC)).then_inc(nodesT_hi_ready, 1)

            def agg_high(l, half):
                act.wait_ge(agg_ready, 2 * l + half + 1)
                cs = slice(half * HC, (half + 1) * HC)
                nc.scalar.copy(aggT_hi[:, cs, :], agg[:, cs, :]).then_inc(agg_hi_ready, 1)

            def high(j):
                g, part = JOBS[j]
                act.wait_ge(in_slot[g % SLOTS], 16 * (g // SLOTS + 1))
                if j >= JSLOTS:
                    act.wait_ge(job_used, j - JSLOTS + 1)
                nc.scalar.copy(w_hi[:, j % JSLOTS, :, :],
                               ring[:, g % SLOTS, part * JU:(part + 1) * JU, :]).then_inc(hi_ready, 1)

            act.wait_ge(consts, 3)
            nc.scalar.activation(spare[:], eps[:], ACT.Sqrt)
            act.wait_ge(onehot_f, 4)
            std_of(0)
            nc.scalar.copy(oh_dstb[:], oh_dst[:]).then_inc(onehot_b, 1)
            turned_relu(0)
            act.wait_ge(ef_psum, 1)
            for k in range(2):
                ins = nc.scalar.copy(ef_sumT[:, k, :], banks[k][:, 0:128])
            ins.then_inc(ef_ready, 1)
            nodesT_high(0, 0)
            high(0)
            nodesT_high(0, 1)
            for j in (1, 2, 3, 4, 5):
                high(j)
            act.wait_ge(in_small, 16)
            for l in range(L):
                j0 = J_L * l
                if l > 0:
                    nodesT_high(l, 1)
                    high(j0 + 4)
                agg_high(l, 0)
                agg_high(l, 1)
                for j in range(j0 + 5 + (l == 0), j0 + 10):
                    high(j)
                std_of(1 + l)
                turned_relu(1 + l, l)
                high(j0 + 10)
                nodesT_high(1 + l, 0)
                high(j0 + 11)
            nodesT_high(L, 1)

            def qkv_out(i, dst):
                act.wait_ge(qkv_psum, i + 1)
                nc.scalar.copy(dst, banks[[0, 1, 2, 3, 0, 1][i]][:, 0:HF]).then_inc(qkv_ready, 1)

            def exps(g):
                act.wait_ge(top_ready, g + 1)
                for h in range(QG):
                    ins = nc.scalar.activation(probs[:, g, h, :], banks[6 + g][:, h * 128:(h + 1) * 128], ACT.Exp,
                                               bias=ntop[:, g, h:h + 1], scale=SCALE,
                                               accum_out=psum_[:, g, h:h + 1])
                ins.then_inc(exp_ready, 1)

            def probsT_out(g):
                act.wait_ge(probsT_psum, g + 1)
                nc.scalar.copy(probsT[:, g, :, :], bank3(4 + g, QG)).then_inc(probsT_ready, 1)

            j0 = J_L * L
            high(j0 + 4)
            high(j0 + 5)
            qkv_out(0, qk[:, 0, :])
            qkv_out(1, qk[:, 1, :])
            high(j0 + 6)
            high(j0 + 7)
            qkv_out(2, qk[:, 2, :])
            high(j0 + 8)
            exps(0)
            high(j0 + 9)
            qkv_out(3, qk[:, 3, :])
            high(j0 + 10)
            qkv_out(4, v[:, 0, :])
            high(j0 + 11)
            probsT_out(0)
            exps(1)
            qkv_out(5, v[:, 1, :])
            probsT_out(1)

            std_of(1 + L)
            turned_relu(1 + L)
            for b in range(NG):
                act.wait_ge(ft_psum, b + 1)
                src = banks[1 + b][:].rearrange("p (c t h o) -> p c t h o", c=2, t=2, h=2)
                nc.scalar.copy(ft[:, 4 * b:4 * b + 4, 0:DH1].rearrange("p (c h) o -> p c h o", c=2),
                               src[:, :, 0, :, :]).then_inc(ft_ready, 1)
                nc.scalar.copy(res[:, 4 * b:4 * b + 4, :].rearrange("p (c h) o -> p c h o", c=2),
                               src[:, :, 1, :, :]).then_inc(res_ready, 1)
            for h in range(NH1):
                if h % ZG == 0:
                    act.wait_ge(nzm_ready, h // ZG + 1)
                nc.scalar.activation(w[:, h, :], zl[:, h, :], ACT.Exp, bias=nzm[:, h:h + 1]).then_inc(w_ready, 1)

        @block.vector
        def _(dve):
            links = [0]

            def link(ins):
                links[0] += 1
                ins.then_inc(vchain, 1)
                dve.wait_ge(vchain, links[0])

            V = nc.vector
            dve.wait_ge(in_bias, 16)
            link(V.tensor_copy(bias_p[:, 0, :], bias_sb[:]))
            link(V.tensor_tensor(bias_r[:, 0, :], bias_sb[:], bias_p[:, 0, :], ALU.subtract))
            link(V.tensor_copy(bias_p[:, 1, :], bias_r[:, 0, :]))
            V.tensor_tensor(bias_p[:, 2, :], bias_r[:, 0, :], bias_p[:, 1, :], ALU.subtract).then_inc(bias_split, 1)

            dve.wait_ge(in_idx, 16)
            dve.wait_ge(consts, 3)
            link(V.tensor_copy(idxf[:], idx_sb[:]))
            for j in range(ET):
                ins = V.tensor_scalar(oh_dst[:, j, :], iota[:], idxf[:, 1, j:j + 1], None, ALU.is_equal)
                if j % 4 == 3:
                    ins.then_inc(onehot_f, 1)

            def stats_half(half, src):
                return V.bn_stats(stats[:, half, :], src)

            def aggregate_stats():
                V.bn_aggr(mv[:], stats[:].rearrange("p a b -> p (a b)")).then_inc(stats_ready, 1)

            def normalise(n, halves):
                dve.wait_ge(std_ready, n + 1)
                link(V.reciprocal(rstd[:], std[:]))
                for half in range(2):
                    V.tensor_scalar(xhat[:, half * HF:(half + 1) * HF], halves[half], mv[:, 0:1], rstd[:, 0:1],
                                    ALU.subtract, ALU.mult).then_inc(xhat_ready, 1)

            dve.wait_ge(in_x, 16)
            link(stats_half(0, x_sb[:, 0:HF]))
            link(stats_half(1, x_sb[:, HF:D]))
            aggregate_stats()
            normalise(0, [x_sb[:, 0:HF], x_sb[:, HF:D]])
            for j in range(ET):
                ins = V.tensor_scalar(oh_srcb[:, j, :], iota[:], idxf[:, 0, j:j + 1], None, ALU.is_equal)
            ins.then_inc(onehot_b, 1)

            dve.wait_ge(count_psum, 1)
            V.tensor_copy(countT[:], banks[6][:, 0:128]).then_inc(count_ready, 1)
            V.tensor_copy(degree[:], banks[2][:, 0:128]).then_inc(count_ready, 1)
            V.tensor_scalar(mask[:], banks[7][:, 0:128], 0.0, MASKED, ALU.is_equal, ALU.mult).then_inc(count_ready, 1)
            dve.wait_ge(count_ready, 2)
            link(V.tensor_tensor(diag[:], ident[:], degree[:], ALU.mult))
            V.tensor_tensor(mixT[:], diag[:], countT[:], ALU.add).then_inc(count_ready, 1)
            dve.wait_ge(vlr_psum, 1)
            dve.wait_ge(wbd_zero, 2)
            for half in range(2):
                rs = slice(half * DH1, (half + 1) * DH1)
                for t in range(2):
                    o = half + NH1 * t
                    V.tensor_copy(vlr[rs, o:o + (C - 1) * 26 + 1:26],
                                  banks[3][rs, o:o + 11:2]).then_inc(vlr_ready, 1)

            def nodes_out(ver, half):
                hs = slice(half * HF, (half + 1) * HF)
                dve.wait_ge(nodes_psum, 2 * ver + half + 1)
                if ver == 0:
                    V.tensor_copy(nodes[:, hs], banks[2 + half][:, 0:HF]).then_inc(nodes_ready, 1)
                else:
                    V.tensor_tensor(nodes[:, hs], banks[2 + half][:, 0:HF], nodes[:, hs],
                                    ALU.add).then_inc(nodes_ready, 1)

            def nodesT_low(ver, half):
                dve.wait_ge(nodesT_hi_ready, 2 * ver + half + 1)
                cs = slice(half * HC, (half + 1) * HC)
                V.tensor_tensor(nodesT_lo[:, cs, :], bank3(4 + half, HC), nodesT_hi[:, cs, :].bitcast(F32),
                                ALU.subtract).then_inc(nodesT_lo_ready, 1)

            def agg_sum(l, half):
                dve.wait_ge(agg_psum, 2 * l + half + 1)
                cs = slice(half * HC, (half + 1) * HC)
                V.tensor_tensor(agg[:, cs, :], bank3(6 + half, HC), edgeT[:, cs, :], ALU.add).then_inc(agg_ready, 1)

            def agg_low(l, half):
                dve.wait_ge(agg_hi_ready, 2 * l + half + 1)
                cs = slice(half * HC, (half + 1) * HC)
                V.tensor_tensor(aggT_lo[:, cs, :], agg[:, cs, :], aggT_hi[:, cs, :].bitcast(F32),
                                ALU.subtract).then_inc(agg_lo_ready, 1)

            def low(j):
                g, part = JOBS[j]
                dve.wait_ge(hi_ready, j + 1)
                V.tensor_tensor(w_lo[:, j % JSLOTS, :, :], ring[:, g % SLOTS, part * JU:(part + 1) * JU, :],
                                w_hi[:, j % JSLOTS, :, :].bitcast(F32), ALU.subtract).then_inc(lo_ready, 1)

            nodes_out(0, 0)
            nodesT_low(0, 0)
            nodes_out(0, 1)
            low(0)
            nodesT_low(0, 1)
            for j in (1, 2, 3, 4, 5):
                low(j)
            dve.wait_ge(edge_psum, 1)
            dve.wait_ge(in_small, 16)
            for c in range(C):
                ins = V.scalar_tensor_tensor(out=edgeT[:, c, :], in0=degree[:], scalar=cols[:, 2 * L, c:c + 1],
                                             in1=banks[6 + c // HC][:, c % HC * 128:(c % HC + 1) * 128],
                                             op0=ALU.mult, op1=ALU.add)
            ins.then_inc(edge_ready, 1)
            dve.wait_ge(edge_ready, 1)
            for l in range(L):
                j0 = J_L * l
                if l > 0:
                    nodesT_low(l, 1)
                agg_sum(l, 0)
                agg_sum(l, 1)
                agg_low(l, 0)
                agg_low(l, 1)
                for j in range(j0 + 4 + 2 * (l == 0), j0 + 8):
                    low(j)
                dve.wait_ge(h1_psum, 2 * l + 1)
                link(stats_half(0, banks[0][:, 0:HF]))
                low(j0 + 8)
                dve.wait_ge(h1_psum, 2 * l + 2)
                link(stats_half(1, banks[1][:, 0:HF]))
                aggregate_stats()
                normalise(1 + l, [banks[0][:, 0:HF], banks[1][:, 0:HF]])
                low(j0 + 9)
                low(j0 + 10)
                nodes_out(1 + l, 0)
                nodesT_low(1 + l, 0)
                low(j0 + 11)
                nodes_out(1 + l, 1)

            nodesT_low(L, 1)
            j0 = J_L * L
            low(j0 + 4)
            dve.wait_ge(nodes_ready, 2 * (L + 1))
            V.tensor_tensor(xn[:], nodes[:], x_sb[:], ALU.add).then_inc(vchain, 1)
            links[0] += 1

            def qkT_out(i):
                dve.wait_ge(qkT_psum, i + 1)
                V.tensor_copy((qT if i % 2 == 0 else kT)[:, i // 2, :, :],
                              banks[4 + i % 2][0:DH0, :].rearrange("p (h n) -> p h n", h=QG)).then_inc(qkT_ready, 1)

            def tops(g):
                dve.wait_ge(score_psum, g + 1)
                link(V.tensor_reduce(top[:, g, :], bank3(6 + g, QG), AX.X, ALU.max))
                V.tensor_scalar(ntop[:, g, :], top[:, g, :], -SCALE, None, ALU.mult).then_inc(top_ready, 1)

            def divide(g):
                dve.wait_ge(exp_ready, g + 1)
                link(V.reciprocal(prec[:, g, :], psum_[:, g, :]))
                V.tensor_tensor(probs[:, g, :, :], probs[:, g, :, :],
                                prec[:, g, :].unsqueeze(2).to_broadcast([128, QG, 128]), ALU.mult).then_inc(probs_ready, 1)

            def attn_out(g):
                dve.wait_ge(attn_psum, g + 1)
                V.tensor_copy(attnT[:, g * QG:(g + 1) * QG, :],
                              banks[2 + g][0:DH0, :].rearrange("p (h n) -> p h n", h=QG)).then_inc(attn_ready, 1)

            low(j0 + 5)
            qkT_out(0)
            qkT_out(1)
            low(j0 + 6)
            low(j0 + 7)
            tops(0)
            low(j0 + 8)
            low(j0 + 9)
            divide(0)
            qkT_out(2)
            qkT_out(3)
            low(j0 + 10)
            low(j0 + 11)
            tops(1)
            divide(1)
            attn_out(0)
            attn_out(1)

            for half in range(2):
                hs = slice(half * HF, (half + 1) * HF)
                dve.wait_ge(o_psum, half + 1)
                link(V.tensor_tensor(x1[:, hs], banks[6 + half][:, 0:HF], xn[:, hs], ALU.add))
                link(stats_half(half, x1[:, hs]))
            aggregate_stats()
            normalise(1 + L, [x1[:, 0:HF], x1[:, HF:D]])
            R = 2 * NH1
            dve.wait_ge(a_psum, 1)
            dve.wait_ge(sels, 3)
            a_bank = banks[0][0:R, 0:128]
            link(V.tensor_copy(a_parts[0:R, :], a_bank))
            link(V.tensor_tensor(a_rest[:], a_bank, a_parts[0:R, :], ALU.subtract))
            V.tensor_copy(a_parts[32:32 + R, :], a_rest[:])
            link(V.tensor_copy(a_mid[:], a_rest[:]))
            V.tensor_tensor(a_parts[64:64 + R, :], a_rest[:], a_mid[:], ALU.subtract).then_inc(a_ready, 1)
            zb = [6, 7, 0]
            tb = [4, 5, 6]

            def leaky(g):
                hs = slice(g * ZG, (g + 1) * ZG)
                dve.wait_ge(z_psum, g + 1)
                link(V.tensor_copy(zl[:, hs, :], bank3(zb[g], ZG)))
                link(V.scalar_tensor_tensor(out=zl[:, hs, :], in0=zl[:, hs, :], scalar=SLOPE, in1=zl[:, hs, :],
                                            op0=ALU.mult, op1=ALU.max))
                V.tensor_reduce(nzm[:, hs], zl[:, hs, :], AX.X, ALU.max, negate=True).then_inc(nzm_ready, 1)

            def weigh(g):
                hs = slice(g * ZG, (g + 1) * ZG)
                dve.wait_ge(wT_psum, g + 1)
                V.tensor_tensor(wT[:, hs, :], bank3(tb[g], ZG),
                                countT[:].unsqueeze(1).to_broadcast([128, ZG, 128]), ALU.mult).then_inc(wT_ready, 1)

            def finish(g):
                hs = slice(g * ZG, (g + 1) * ZG)
                dve.wait_ge(gagg_psum, g + 1)
                b = banks[1 + g][:, 0:ZG * (DH1 + 1)].rearrange("p (h o) -> p h o", h=ZG)
                link(V.tensor_scalar(den[:, hs], b[:, :, DH1], 1e-16, None, ALU.max))
                link(V.reciprocal(rden[:, hs], den[:, hs]))
                link(V.tensor_tensor(agg1[:, hs, :], b[:, :, 0:DH1],
                                     rden[:, hs].unsqueeze(2).to_broadcast([128, ZG, DH1]), ALU.mult))
                dve.wait_ge(res_ready, NG)
                link(V.tensor_tensor(agg1[:, hs, :], agg1[:, hs, :], res[:, hs, :], ALU.add))
                cs = slice(g * ZG * DH1, (g + 1) * ZG * DH1)
                V.scalar_tensor_tensor(out=y[:, cs], in0=agg1[:, hs, :].rearrange("p h o -> p (h o)"), scalar=0.0,
                                       in1=x1[:, cs], op0=ALU.max, op1=ALU.add).then_inc(y_ready, 1)

            leaky(0)
            leaky(1)
            weigh(0)
            leaky(2)
            weigh(1)
            finish(0)
            weigh(2)
            finish(1)
            finish(2)


def kernel(**inputs):
    import numpy as np
    import concourse.bacc as bacc
    from concourse.bass_utils import run_bass_kernel_spmd as run

    a = {k: np.asarray(v) for k, v in inputs.items()}

    def units(w):
        o, i = w.shape
        return w.T.reshape(i // 128, 128, o // HF, HF).transpose(2, 0, 1, 3)

    pre = "L0_gnn_"
    flat = lambda u: u.reshape(-1, 128, HF)
    stream = [flat(units(a[pre + "Wn"]))]
    for l in range(L):
        u = units(a[pre + "W1"][l])
        stream += [u[0, 0:HC], u[1, 0:HC], u[0, HC:C], u[1, HC:C], u[0, C:], u[1, C:]]
        stream += [flat(units(a[pre + "W2"][l]))]
    q0, q1, k0, k1, v0, v1 = units(a[pre + "Wqkv"])
    stream += [q0[0:HC], k0[0:HC], q0[HC:C], k0[HC:C], q1, k1, v0, v1]
    stream = np.concatenate(stream)
    twice = lambda m: np.concatenate([m, m])
    arrays = {
        "x": a["x"],
        "idx": np.stack([a["src"].reshape(128, ET), a["dst"].reshape(128, ET)], 1),
        "ef": a["edge_attr_256"].reshape(128, ET, DE),
        "wstream": stream.reshape(GROUPS, GU, 128, HF).transpose(0, 2, 1, 3),
        "we": a[pre + "We"].T.reshape(DE // 128, 128, D).transpose(1, 0, 2),
        "wo": a[pre + "Wo"].T.reshape(NH0, DH0, D).transpose(1, 0, 2),
        "biases": np.concatenate([a[pre + n].reshape(-1) for n in ("b1", "b2", "bo", "bqkv")]).reshape(BR, 128),
        "small_in": np.concatenate([
            np.concatenate([a[pre + n].reshape(-1, C, 128) for n in ("ln_g", "ln_b", "be")]).transpose(2, 0, 1)
            .reshape(128, -1),
            twice(a["L1_gnn_W"]), twice(a["L1_gnn_W"]),
            twice(a["L1_gnn_attn_l"][0].T), twice(a["L1_gnn_attn_r"][0].T),
            twice(a["L1_gnn_W"].T), twice(a["L1_gnn_W_res"].T)], 1),
        "bn": a[pre + "bn"].reshape(1, D),
    }
    arrays = {k: np.ascontiguousarray(v) for k, v in arrays.items()}
    nc = bacc.Bacc("TRN2", target_bir_lowering=False, num_devices=1)
    args = [nc.dram_tensor(k, v.shape, mybir.dt.from_np(v.dtype), kind="ExternalInput").ap() for k, v in arrays.items()]
    out = nc.dram_tensor("out", (N, D), F32, kind="ExternalOutput").ap()
    build(nc, *args, out)
    r = run(nc, [arrays], core_ids=[0])
    return r.results[0]["out"]
```

```python
from contextlib import ExitStack

import concourse.bass as bass
from concourse import mybir

ALU = mybir.AluOpType
ACT = mybir.ActivationFunctionType
AX = mybir.AxisListType
F32 = mybir.dt.float32
F32R = mybir.dt.float32r
BF16 = mybir.dt.bfloat16
I32 = mybir.dt.int32

N = 128
D = 768
DE = 256
E = 2048
L = 3
C = D // 128
HC = C // 2
HF = D // 2
ET = E // 128
EF_LOADS = (0, 4, 8, 12, ET)
NH0, DH0 = 8, 96
NH1, DH1 = 12, 64
QG = HF // DH0
ZG = 4
NG = NH1 // ZG
Z_BANKS, T_BANKS = (6, 7, 0), (4, 5, 6)
EPS = 1e-5
WARM, REST = 42, 24
SCALE = DH0 ** -0.5
SLOPE = 0.2
MASKED = -1e30

JU = 3
GU = 2 * JU
SLOTS = 8
JSLOTS = 4
G_N = 2
G_1, G_2 = 4, 2
G_L = G_1 + G_2
G_QKV = 6
GROUPS = G_N + L * G_L + G_QKV
J_N, J_1, J_L = 2 * G_N, 2 * G_1, 2 * G_L
JOBS = 2 * GROUPS
QKV_JOB = (2, 3, 5, 7, 9, 11)
PIECES = [[(0, 3, 4), (3, 6, 5)]] + L * [[(0, 1, 4), (1, 3, 5), (3, 6, 7)]] + [[(0, 1, 4), (1, 3, 5), (3, 6, 1)]]
BIAS = {"1": (0, 0), "n": (0, L * D), "2": (32, 0), "o": (32, L * D), "qkv": (64, 0)}
BW = (L + 1) * D
BT = 5 * D + 2 * L * D
BR = BT // 128


def build(nc, x, idx, ef, wstream, we, wo, biases, small_in, out):
    ctx = ExitStack()
    with ctx:
        def sb(name, shape, dt=F32):
            return ctx.enter_context(nc.sbuf_tensor(name, shape, dt))

        def sem(name):
            return ctx.enter_context(nc.semaphore(name))

        banks = [ctx.enter_context(nc.psum_tensor(f"bank{i}", [128, 512], F32)) for i in range(8)]

        ring = sb("ring", [128, SLOTS, GU, HF])
        we_sb = sb("we_sb", [128, DE // 128, D])
        wo_slot = GROUPS % SLOTS
        wo_slots = -(-NH0 * D // (GU * HF))
        assert wo_slot + wo_slots <= SLOTS
        wo_sb = ring[0:DH0].rearrange("p s u f -> p (s u f)")[
            :, wo_slot * GU * HF:wo_slot * GU * HF + NH0 * D].rearrange("p (h f) -> p h f", h=NH0)
        shared = sb("shared", [128, ET * DE + ET * 128 + ET * 64 + ET * 64])
        taken = {"early": 0, "late": 0}

        def share(when, shape, dt=F32):
            size = 1
            for s in shape[1:]:
                size *= s
            words = size if dt == F32 else (size + 1) // 2
            flat = shared[0:shape[0], taken[when]:taken[when] + words]
            taken[when] += words
            if dt != F32:
                flat = flat.bitcast(dt)[:, 0:size]
            if len(shape) == 3:
                return flat.rearrange("p (a b) -> p a b", a=shape[1])
            if len(shape) == 4:
                return flat.rearrange("p (a b c) -> p a b c", a=shape[1], b=shape[2])
            return flat

        ef_sb = share("early", [128, ET, DE])
        late_at = [(wo_slot + wo_slots) * GU * HF]

        def late(shape):
            size = shape[1] * (shape[2] if len(shape) == 3 else 1)
            flat = ring[0:shape[0]].rearrange("p s u f -> p (s u f)")[:, late_at[0]:late_at[0] + size]
            late_at[0] += size
            assert late_at[0] <= SLOTS * GU * HF
            return flat if len(shape) == 2 else flat.rearrange("p (a b) -> p a b", a=shape[1])

        w_hi = sb("w_hi", [128, JSLOTS, JU, HF], F32R)
        w_lo = sb("w_lo", [128, JSLOTS, JU, HF], F32R)
        x_sb = sb("x_sb", [128, D])
        idx_sb = sb("idx_sb", [128, 2, ET], I32)
        idxf = sb("idxf", [128, 2, ET])
        iota = sb("iota", [128, 128], BF16)
        ident = sb("ident", [128, 128])
        identb = sb("identb", [128, 128], BF16)
        ones = sb("ones", [128, 128], BF16)
        ones_f = sb("ones_f", [128, 128])
        eps = sb("eps", [128, 1])
        oh_dst = share("early", [128, ET, 128])
        oh_dstb = share("early", [128, ET, 128], BF16)
        oh_srcb = share("early", [128, ET, 128], BF16)
        ef_sumT = sb("ef_sumT", [128, DE // 128, 128])
        countT = sb("countT", [128, 128])
        degree = sb("degree", [128, 128])
        diag = sb("diag", [128, 128])
        mixT = sb("mixT", [128, 128])
        mask = sb("mask", [128, 128], BF16)
        edgeT = sb("edgeT", [128, C, 128])
        SMALL = {"cols": (2 * L + 1) * C, "w2x": 2 * DH1, "attn": 2 * NH1, "wt": 2 * DH1}
        small = sb("small", [128, sum(SMALL.values())])
        at, small_at = 0, {}
        for name, width in SMALL.items():
            small_at[name] = small[:, at:at + width]
            at += width
        cols = small_at["cols"].rearrange("p (a c) -> p a c", c=C)
        w2x = small_at["w2x"][0:DH1]
        attn_lr = small_at["attn"][0:DH1]
        wt2 = small_at["wt"].rearrange("p (t o) -> p t o", t=2)
        bias_sb = sb("bias_sb", [BR, 128])
        bias_p = sb("bias_p", [BR, 3, 128], BF16)
        bias_r = sb("bias_r", [BR, 2, 128])
        brow = sb("brow", [64 + 3, BW], BF16)
        stats = sb("stats", [128, 2, 6])
        mv = sb("mv", [128, 2])
        std = sb("std", [128, 1])
        spare = sb("spare", [128, 1])
        rstd = sb("rstd", [128, 1])
        xhat = sb("xhat", [128, D])
        hT = sb("hT", [128, C, 128])
        nodes = sb("nodes", [128, D])
        nodesT_hi = sb("nodesT_hi", [128, C, 128], F32R)
        nodesT_lo = sb("nodesT_lo", [128, C, 128], F32R)
        agg = xhat[:].rearrange("p (c n) -> p c n", c=C)
        aggT_hi = sb("aggT_hi", [128, C, 128], F32R)
        aggT_lo = sb("aggT_lo", [128, C, 128], F32R)
        hT_hi, hT_lo = aggT_hi, aggT_lo
        qk = share("late", [128, 4, HF])
        v = share("late", [128, 2, HF])
        qT = we_sb[0:DH0].rearrange("p a d -> p (a d)")[:, 0:2 * QG * 128].rearrange(
            "p (g h n) -> p g h n", g=2, h=QG)
        kT = sb("kT", [DH0, 2, QG, 128])
        top = sb("top", [128, 2, QG])
        ntop = sb("ntop", [128, 2, QG])
        probs = share("late", [128, 2, QG, 128])
        psum_ = sb("psum_", [128, 2, QG])
        prec = sb("prec", [128, 2, QG])
        probsT = share("late", [128, 2, QG, 128])
        attnT_hi = [t[0:DH0, 0:QG, :] for t in (aggT_hi, nodesT_hi)]
        attnT_lo = [t[0:DH0, 0:QG, :] for t in (aggT_lo, nodesT_lo)]
        wo_hi, wo_lo = (t[0:DH0].rearrange("p s u f -> p (s u) f").rearrange("p (k h) f -> p k h f", h=QG)
                        for t in (w_hi, w_lo))
        xn = share("late", [128, D])
        x1 = late([128, D])
        wbd = sb("wbd", [128, 2, 128])
        vlr = sb("vlr", [128, C * 2 * NH1])
        a_parts = sb("a_parts", [96, 128], BF16)
        a_mid = sb("a_mid", [2 * NH1, 128], BF16)
        a_rest = sb("a_rest", [2 * NH1, 128])
        sel_l = sb("sel_l", [96, NH1, 128], BF16)
        sel_r = sb("sel_r", [96, NH1, 128], BF16)
        ft = late([128, NH1, DH1 + 1])
        res = late([128, NH1, DH1])
        zl = share("late", [128, NH1, 128])
        nzm = sb("nzm", [128, NH1])
        w = share("late", [128, NH1, 128])
        wT = late([128, NH1, 128])
        den = sb("den", [128, NH1])
        rden = sb("rden", [128, NH1])
        y = late([128, D])

        in_x, in_idx, in_we, in_wo, in_small, in_bias = map(
            sem, ["in_x", "in_idx", "in_we", "in_wo", "in_small", "in_bias"])
        in_brow = [sem(f"in_brow{i}") for i in range(3)]
        in_ef = [sem(f"in_ef{i}") for i in range(4)]
        in_slot = [sem(f"in_slot{i}") for i in range(SLOTS)]
        hi_ready, lo_ready, job_used = sem("hi_ready"), sem("lo_ready"), sem("job_used")
        pool_step = sem("pool_step")
        consts, ones_ready, wbd_ready = sem("consts"), sem("ones_ready"), sem("wbd_ready")
        ft_ones = sem("ft_ones")
        identb_ready, a_parts_zero = sem("identb_ready"), sem("a_parts_zero")
        dve_step = sem("dve_step")
        onehot_f, onehot_b = sem("onehot_f"), sem("onehot_b")
        bias_split = sem("bias_split")
        ef_psum, count_psum, vlr_psum = sem("ef_psum"), sem("count_psum"), sem("vlr_psum")
        mix_ready = sem("mix_ready")
        ef_ready, count_ready, vlr_ready = sem("ef_ready"), sem("count_ready"), sem("vlr_ready")
        wbd_zero = sem("wbd_zero")
        edge_psum, edge_ready = sem("edge_psum"), sem("edge_ready")
        stats_ready, std_ready, xhat_ready = sem("stats_ready"), sem("std_ready"), sem("xhat_ready")
        xhatT_psum, hT_ready = sem("xhatT_psum"), sem("hT_ready")
        hT_hi_ready, hT_lo_ready = sem("hT_hi_ready"), sem("hT_lo_ready")
        nodes_ready = sem("nodes_ready")
        nodesT_psum, nodesT_hi_ready, nodesT_lo_ready = sem("nodesT_psum"), sem("nodesT_hi_ready"), sem("nodesT_lo_ready")
        agg_psum, agg_ready = sem("agg_psum"), sem("agg_ready")
        agg_hi_ready, agg_lo_ready = sem("agg_hi_ready"), sem("agg_lo_ready")
        qkv_ready = sem("qkv_ready")
        qkT_psum, qkT_ready = sem("qkT_psum"), sem("qkT_ready")
        score_psum, top_ready, exp_ready = sem("score_psum"), sem("top_ready"), sem("exp_ready")
        probs_ready, probsT_psum, probsT_ready = sem("probs_ready"), sem("probsT_psum"), sem("probsT_ready")
        attn_psum, attn_hi_ready, attn_lo_ready = sem("attn_psum"), sem("attn_hi_ready"), sem("attn_lo_ready")
        wo_hi_ready, wo_lo_ready, wo_used = sem("wo_hi_ready"), sem("wo_lo_ready"), sem("wo_used")
        xn_ready, x1_ready = sem("xn_ready"), sem("x1_ready")
        a_psum, a_ready = sem("a_psum"), sem("a_ready")
        ft_psum, ft_ready, res_ready = sem("ft_psum"), sem("ft_ready"), sem("res_ready")
        z_psum, slope_ready, nzm_ready, w_ready = sem("z_psum"), sem("slope_ready"), sem("nzm_ready"), sem("w_ready")
        wT_psum, wT_ready = sem("wT_psum"), sem("wT_ready")
        gagg_psum, rden_ready, scaled = sem("gagg_psum"), sem("rden_ready"), sem("scaled")
        y0_ready, y_ready, stored = sem("y0_ready"), sem("y_ready"), sem("stored")

        def bank3(b, n):
            return banks[b][:, 0:n * 128].rearrange("p (c n) -> p c n", c=n)

        def nodes_done(ver, half):
            first = 0 if ver == 0 else J_N + J_L * (ver - 1) + J_1
            return first + 3 + half

        def pieces_before(n):
            return sum(len(p) for p in PIECES[:n])

        def turned(n, c):
            for i, (a, b, bank) in enumerate(PIECES[n]):
                if a <= c < b:
                    return pieces_before(n) + i, banks[bank][:, (c - a) * 128:(c - a + 1) * 128]

        def wo_chunk(k):
            return wo_sb[:, k // 2 * QG:(k // 2 + 1) * QG, k % 2 * HF:(k % 2 + 1) * HF]

        block = ctx.enter_context(nc.Block())

        @block.sync
        def _(sp):
            def load(g):
                if g >= SLOTS:
                    sp.wait_ge(lo_ready, 2 * (g - SLOTS) + 2)
                sp.dma_start(ring[:, g % SLOTS, :, :], wstream[g]).then_inc(in_slot[g % SLOTS], 16)

            sp.dma_start(idx_sb[:], idx).then_inc(in_idx, 16)
            for i in range(4):
                es = slice(EF_LOADS[i], EF_LOADS[i + 1])
                sp.dma_start(ef_sb[:, es, :], ef[:, es, :]).then_inc(in_ef[i], 16)
                if i == 0:
                    sp.dma_start(x_sb[:], x).then_inc(in_x, 16)
                if i == 2:
                    load(0)
            for g in range(1, G_N):
                load(g)
            sp.wait_ge(bias_split, 1)
            r = 0
            for i, rows in enumerate(((L + 1) * C, (L + 1) * C, L * C)):
                for p in range(3):
                    sp.dma_start(brow[32 * i + p:32 * i + p + 1, 0:rows * 128].rearrange("o (r n) -> o r n", n=128),
                                 bias_p[r:r + rows, p, :]).then_inc(in_brow[i], 16)
                r += rows
            sp.dma_start(we_sb[:], we).then_inc(in_we, 16)
            for g in range(G_N, GROUPS):
                load(g)
            for i in range(wo_slots):
                sp.wait_ge(lo_ready, 2 * (GROUPS - SLOTS + i) + 2)
            sp.dma_start(wo_sb[:], wo).then_inc(in_wo, 16)
            for g in (1, 0, 2):
                sp.wait_ge(y0_ready if g == 0 else y_ready, max(g, 1))
                cs = slice(g * ZG * DH1, (g + 1) * ZG * DH1)
                sp.dma_start(out[:, cs], y[:, cs]).then_inc(stored, 16)
            sp.wait_ge(stored, 16 * NG)

        @block.gpsimd
        def _(pool):
            nc.gpsimd.iota(iota[:], [[1, 128]], base=0, channel_multiplier=0,
                           allow_small_or_imprecise_dtypes=True).then_inc(consts, 1)
            nc.gpsimd.memset(ones[:], 1.0).then_inc(ones_ready, 1)
            nc.gpsimd.memset(ones_f[:], 1.0).then_inc(ones_ready, 1)
            nc.gpsimd.memset(eps[:], EPS).then_inc(consts, 1)
            nc.gpsimd.memset(ident[:], 0.0).then_inc(pool_step, 1)
            pool.wait_ge(pool_step, 1)
            nc.gpsimd.affine_select(out=ident[:], in_=ident[:], compare_op=ALU.not_equal, fill=1.0, base=0,
                                    pattern=[[-1, 128]], channel_multiplier=1).then_inc(consts, 1)
            nc.gpsimd.memset(wbd[:], 0.0).then_inc(wbd_zero, 1)
            nc.gpsimd.memset(vlr[:], 0.0).then_inc(wbd_zero, 1)
            pool.wait_ge(consts, 3)
            nc.gpsimd.tensor_copy(identb[:], ident[:]).then_inc(identb_ready, 1)

            def attention_constants():
                pool.wait_ge(in_small, 16)
                pool.wait_ge(wbd_zero, 1)
                for half in range(2):
                    rs = slice(half * DH1, (half + 1) * DH1)
                    if half:
                        pool.wait_ge(wbd_ready, half)
                    nc.gpsimd.tensor_copy(wbd[rs, :, rs], wt2[rs, :, :]).then_inc(wbd_ready, 1)
                pool.wait_ge(wbd_ready, 2)
                nc.gpsimd.memset(sel_l[:], 0.0).then_inc(pool_step, 1)
                nc.gpsimd.memset(sel_r[:], 0.0).then_inc(pool_step, 1)
                nc.gpsimd.memset(a_parts[:], 0.0).then_inc(a_parts_zero, 1)
                n = 3
                for part in range(3):
                    for t, off in ((sel_l, 0), (sel_r, NH1)):
                        pool.wait_ge(pool_step, n)
                        nc.gpsimd.affine_select(out=t[:], in_=t[:], compare_op=ALU.not_equal, fill=1.0,
                                                base=-32 * part - off, pattern=[[-1, NH1], [0, 128]],
                                                channel_multiplier=1).then_inc(pool_step, 1)
                        n += 1

            def agg_low(l, half):
                pool.wait_ge(agg_hi_ready, 2 * l + half + 1)
                cs = slice(half * HC, (half + 1) * HC)
                nc.gpsimd.tensor_tensor(aggT_lo[:, cs, :], agg[:, cs, :], aggT_hi[:, cs, :].bitcast(F32),
                                        ALU.subtract).then_inc(agg_lo_ready, 1)

            for l in range(L):
                agg_low(l, 0)
                agg_low(l, 1)
                if l == 0:
                    attention_constants()
            pool.wait_ge(nodes_ready, 2 * (L + 1))
            nc.gpsimd.tensor_tensor(xn[:], nodes[:], x_sb[:], ALU.add).then_inc(xn_ready, 1)
            pool.wait_ge(lo_ready, JOBS)
            nc.gpsimd.memset(ft[:, :, DH1:DH1 + 1], 1.0).then_inc(ft_ones, 1)
            pool.wait_ge(scaled, 1)
            pool.wait_ge(x1_ready, 2)
            cs = slice(0, ZG * DH1)
            nc.gpsimd.tensor_tensor(y[:, cs], y[:, cs], res[:, 0:ZG, :].rearrange("p h o -> p (h o)"),
                                    ALU.add).then_inc(scaled, 1)
            pool.wait_ge(scaled, 2)
            nc.gpsimd.tensor_scalar(y[:, cs], y[:, cs], 0.0, None, ALU.max).then_inc(scaled, 1)
            pool.wait_ge(scaled, 3)
            nc.gpsimd.tensor_tensor(y[:, cs], y[:, cs], x1[:, cs], ALU.add).then_inc(y0_ready, 1)

        @block.tensor
        def _(pe):
            def bias(bank, name, at, start=False):
                p, c = BIAS[name]
                pe.wait_ge(in_brow[p // 32], 48)
                pe.matmul(bank[:, 0:HF], ones[p:p + 3, :], brow[p:p + 3, c + at:c + at + HF],
                          start=start, stop=False)

            def products_hi(bank, j, his, his_ready=None, before=0, start=False):
                js = j % JSLOTS
                pe.wait_ge(hi_ready, j + 1)
                for i in range(JU):
                    if his_ready is not None:
                        pe.wait_ge(his_ready, before + i + 1)
                    pe.matmul(bank[:, 0:HF], his[i], w_hi[:, js, i, :], start=start and i == 0, stop=False)
                pe.wait_ge(lo_ready, j + 1)
                for i in range(JU):
                    pe.matmul(bank[:, 0:HF], his[i], w_lo[:, js, i, :], start=False, stop=False)

            def products_lo(bank, j, los, act_lo, stop=False):
                pe.wait_ge(*act_lo)
                for i in range(JU):
                    mm = pe.matmul(bank[:, 0:HF], los[i], w_hi[:, j % JSLOTS, i, :],
                                   start=False, stop=stop and i == JU - 1)
                mm.then_inc(job_used, 1)

            def products(bank, j, his, los, act_lo, stop=False):
                products_hi(bank, j, his)
                products_lo(bank, j, los, act_lo, stop)

            def keep_warm(bank, n):
                for _ in range(n):
                    pe.matmul(banks[bank][:, 0:128], ones[:], ones[:], start=True, stop=True)

            pe.wait_ge(ones_ready, 1)
            keep_warm(5, WARM)

            def xhat_turn(n):
                for i, (a, b, _) in enumerate(PIECES[n]):
                    pe.wait_ge(xhat_ready, pieces_before(n) + i + 1)
                    for c in range(a, b):
                        mm = pe.transpose(turned(n, c)[1], xhat[:, c * 128:(c + 1) * 128], ident[:])
                    mm.then_inc(xhatT_psum, 1)

            def nodes_turn(ver, half):
                pe.wait_ge(nodes_ready, 2 * ver + half + 1)
                for c in range(half * HC, (half + 1) * HC):
                    mm = pe.transpose(banks[4 + half][:, c % HC * 128:(c % HC + 1) * 128],
                                      nodes[:, c * 128:(c + 1) * 128], ident[:])
                mm.then_inc(nodesT_psum, 1)

            def edge_features(js):
                for j in js:
                    if j in EF_LOADS:
                        pe.wait_ge(onehot_f, EF_LOADS.index(j) + 1)
                        pe.wait_ge(in_ef[EF_LOADS.index(j)], 16)
                    for k in range(2):
                        mm = pe.matmul(banks[k][:, 0:128], ef_sb[:, j, k * 128:(k + 1) * 128],
                                       oh_dst[:, j, :], start=j == 0, stop=j == ET - 1)
                return mm

            def nodes_shift(ver):
                for half in range(2):
                    if ver > 0:
                        bias(banks[2 + half], "2", (ver - 1) * D + half * HF, start=True)
                    else:
                        bias(banks[2 + half], "n", half * HF)

            def nodes_product(ver, j0):
                def passes_hi(half, part):
                    products_hi(banks[2 + half], j0 + 2 * part + half,
                                [hT_hi[:, part * HC + i, :] for i in range(HC)],
                                hT_hi_ready, C * ver + part * HC, start=ver == 0 and part == 0)

                def passes_lo(half, part):
                    products_lo(banks[2 + half], j0 + 2 * part + half,
                                [hT_lo[:, part * HC + i, :] for i in range(HC)], (hT_lo_ready, 2 * ver + part + 1),
                                stop=part == 1)

                passes_hi(0, 0)
                passes_hi(1, 0)
                if ver == 0:
                    turn_counts()
                    nodes_shift(0)
                passes_lo(0, 0)
                passes_lo(1, 0)
                passes_hi(0, 1)
                passes_lo(0, 1)
                if ver == 0:
                    edges_product()
                passes_hi(1, 1)
                nodes_turn(ver, 0)
                passes_lo(1, 1)

            def turn_counts():
                pe.wait_ge(count_ready, 1)
                pe.wait_ge(in_small, 16)
                pe.transpose(banks[7][:, 0:128], countT[:], ident[:])
                pe.matmul(banks[7][:, 256:256 + 2 * NH1], w2x, attn_lr, start=True, stop=True)
                pe.wait_ge(ones_ready, 2)
                pe.matmul(banks[7][:, 128:256], ones_f[:], countT[:], start=True, stop=True).then_inc(vlr_psum, 1)

            def edges_product():
                pe.wait_ge(in_we, 16)
                pe.wait_ge(ef_ready, 1)
                pe.wait_ge(count_ready, 3)
                pe.wait_ge(vlr_ready, 4)
                for c in range(C):
                    o = banks[6 + c // HC][:, c % HC * 128:(c % HC + 1) * 128]
                    cs = slice(c * 128, (c + 1) * 128)
                    pe.matmul(o, we_sb[:, 0, cs], ef_sumT[:, 0, :], start=True, stop=False)
                    mm = pe.matmul(o, we_sb[:, 1, cs], ef_sumT[:, 1, :], start=False, stop=True)
                    if c % HC == HC - 1:
                        mm.then_inc(edge_psum, 1)

            def nodes_job(bank, ver, j, part, stop=False):
                ks = range(part * HC, (part + 1) * HC)
                pe.wait_ge(nodesT_hi_ready, 2 * ver + part + 1)
                products(bank, j, [nodesT_hi[:, k, :] for k in ks], [nodesT_lo[:, k, :] for k in ks],
                         (nodesT_lo_ready, 2 * ver + part + 1), stop)

            def aggregate(l, half):
                if l == 0:
                    pe.wait_ge(mix_ready, 1)
                    pe.wait_ge(edge_ready, half + 1)
                elif half == 0:
                    pe.wait_ge(agg_ready, 2 * l)
                for c in range(half * HC, (half + 1) * HC):
                    mm = pe.matmul(banks[6 + half][:, c % HC * 128:(c % HC + 1) * 128],
                                   nodes[:, c * 128:(c + 1) * 128], mixT[:], start=True, stop=True)
                mm.then_inc(agg_psum, 1)

            def agg_job(bank, l, j, part):
                ks = range(part * HC, (part + 1) * HC)
                pe.wait_ge(agg_hi_ready, 2 * l + part + 1)
                products(bank, j, [aggT_hi[:, k, :] for k in ks], [aggT_lo[:, k, :] for k in ks],
                         (agg_lo_ready, 2 * l + part + 1), stop=part == 1)

            edge_features(range(0, ET // 2))
            pe.wait_ge(consts, 3)
            xhat_turn(0)
            edge_features(range(ET // 2, ET - 4))
            pe.wait_ge(onehot_b, 2)
            for j in range(ET):
                mm = pe.matmul(banks[6][:, 0:128], oh_srcb[:, j, :], oh_dstb[:, j, :], start=j == 0, stop=j == ET - 1)
            mm.then_inc(count_psum, 1)
            edge_features(range(ET - 4, ET)).then_inc(ef_psum, 1)
            nodes_product(0, 0)

            for l in range(L):
                j0 = J_N + J_L * l
                h0, h1 = banks[0], banks[1]
                if l == 0:
                    pe.wait_ge(ef_ready, 1)
                bias(h0, "1", l * D, start=True)
                bias(h1, "1", l * D + HF, start=True)
                nodes_job(h0, l, j0, 0)
                nodes_turn(l, 1)
                aggregate(l, 0)
                aggregate(l, 1)
                nodes_job(h1, l, j0 + 1, 0)
                nodes_job(h0, l, j0 + 2, 1)
                nodes_job(h1, l, j0 + 3, 1)
                for half in range(2):
                    bank = banks[half]
                    agg_job(bank, l, j0 + 4 + 2 * half, 0)
                    agg_job(bank, l, j0 + 5 + 2 * half, 1)
                nodes_shift(1 + l)
                keep_warm(6, REST - 6)
                xhat_turn(1 + l)
                nodes_product(1 + l, j0 + J_1)

            j0 = J_N + J_L * L
            qkv_banks = [banks[i] for i in (0, 1, 2, 3, 0, 1)]

            def project(i, part, job):
                if i >= 4 and part == 0:
                    pe.wait_ge(qkv_ready, i - 3)
                if part == 0 and i != 1:
                    for k in (0, 1) if i == 0 else (i,):
                        bias(qkv_banks[k], "qkv", [0, D, HF, D + HF, 2 * D, 2 * D + HF][k], start=True)
                assert part == 0 or job == QKV_JOB[i]
                nodes_job(qkv_banks[i], L, j0 + job, part, stop=part == 1)

            def turn_qk(i):
                pe.wait_ge(qkv_ready, i + 1)
                if i >= 2:
                    pe.wait_ge(qkT_ready, i - 1)
                for h in range(QG):
                    mm = pe.transpose(banks[4 + i % 2][0:DH0, h * 128:(h + 1) * 128],
                                      qk[:, i, h * DH0:(h + 1) * DH0], ident[:])
                mm.then_inc(qkT_psum, 1)

            def scores(g):
                pe.wait_ge(qkT_ready, 2 * g + 2)
                for h in range(QG):
                    mm = pe.matmul(banks[6 + g][:, h * 128:(h + 1) * 128], qT[:, g, h, :], kT[:, g, h, :],
                                   start=True, stop=True)
                mm.then_inc(score_psum, 1)

            def turn_probs(g):
                pe.wait_ge(probs_ready, g + 1)
                pe.wait_ge(qkT_ready, 4)
                for h in range(QG):
                    mm = pe.transpose(banks[4 + g][:, h * 128:(h + 1) * 128], probs[:, g, h, :], ident[:])
                mm.then_inc(probsT_psum, 1)

            def attend(g):
                pe.wait_ge(probsT_ready, g + 1)
                pe.wait_ge(qkv_ready, 5 + g)
                for h in range(QG):
                    mm = pe.matmul(banks[2 + g][0:DH0, h * 128:(h + 1) * 128], v[:, g, h * DH0:(h + 1) * DH0],
                                   probsT[:, g, h, :], start=True, stop=True)
                mm.then_inc(attn_psum, 1)

            def start_out(half):
                pe.wait_ge(exp_ready, half + 1)
                pe.wait_ge(xn_ready, 1)
                pe.matmul(banks[6 + half][:, 0:HF], ident[:], xn[:, half * HF:(half + 1) * HF],
                          start=True, stop=False)
                bias(banks[6 + half], "o", half * HF)

            def project_out(half, g):
                bank, k = banks[6 + half], 2 * g + half
                pe.wait_ge(attn_hi_ready, g + 1)
                pe.wait_ge(wo_hi_ready, k + 1)
                for h in range(QG):
                    pe.matmul(bank[:, 0:HF], attnT_hi[g][:, h, :], wo_hi[:, k % 3, h, :],
                              start=False, stop=False)
                pe.wait_ge(wo_lo_ready, k + 1)
                for h in range(QG):
                    pe.matmul(bank[:, 0:HF], attnT_hi[g][:, h, :], wo_lo[:, k % 3, h, :],
                              start=False, stop=False)
                pe.wait_ge(attn_lo_ready, g + 1)
                for h in range(QG):
                    mm = pe.matmul(bank[:, 0:HF], attnT_lo[g][:, h, :], wo_hi[:, k % 3, h, :],
                                   start=False, stop=g == 1 and h == QG - 1)
                mm.then_inc(wo_used, 1)

            project(0, 0, 0)
            nodes_turn(L, 1)
            project(1, 0, 1)
            project(0, 1, 2)
            project(1, 1, 3)
            project(2, 0, 4)
            turn_qk(0)
            turn_qk(1)
            project(2, 1, 5)
            scores(0)
            project(3, 0, 6)
            project(3, 1, 7)
            project(4, 0, 8)
            turn_qk(2)
            turn_qk(3)
            project(4, 1, 9)
            scores(1)
            turn_probs(0)
            project(5, 0, 10)
            project(5, 1, 11)
            attend(0)
            start_out(0)
            start_out(1)
            turn_probs(1)
            project_out(0, 0)
            attend(1)
            project_out(1, 0)
            project_out(0, 1)
            project_out(1, 1)

            keep_warm(0, REST)
            xhat_turn(1 + L)
            keep_warm(0, 6)
            for c in range(C):
                pe.wait_ge(hT_ready, C * (1 + L) + c + 1)
                mm = pe.matmul(banks[0][0:2 * NH1, 0:128], vlr[:, c * 2 * NH1:(c + 1) * 2 * NH1], hT[:, c, :],
                               start=c == 0, stop=c == C - 1)
            mm.then_inc(a_psum, 1)

            def gat_features(c):
                o = banks[1 + c // 2][:, c % 2 * 256:c % 2 * 256 + 256]
                mm = pe.matmul(o, hT[:, c, :], wbd[:], start=True, stop=True)
                if c % 2 == 1:
                    mm.then_inc(ft_psum, 1)

            def edge_mask(g):
                pe.matmul(bank3(Z_BANKS[g], ZG), identb[:], mask[:].unsqueeze(1).to_broadcast([128, ZG, 128]),
                          start=True, stop=False)

            def gat_scores(g):
                bank = banks[Z_BANKS[g]]
                hs = slice(g * ZG, (g + 1) * ZG)
                pe.matmul(bank3(Z_BANKS[g], ZG), a_parts[:], sel_r[:, hs, :], start=False, stop=False)
                for h in range(ZG):
                    mm = pe.matmul(bank[:, h * 128:(h + 1) * 128], sel_l[:, g * ZG + h, :], a_parts[:],
                                   start=False, stop=h == ZG - 1)
                mm.then_inc(z_psum, 1)

            pe.wait_ge(wbd_ready, 2)
            pe.wait_ge(qkv_ready, 6)
            pe.wait_ge(attn_lo_ready, 2)
            for c in range(2):
                gat_features(c)
            pe.wait_ge(identb_ready, 1)
            pe.wait_ge(pool_step, 3 + 6)
            pe.wait_ge(x1_ready, 2)
            for g in range(2):
                edge_mask(g)
            pe.wait_ge(a_ready, 1)
            gat_scores(0)
            gat_scores(1)
            edge_mask(2)
            gat_scores(2)
            for c in range(2, C):
                gat_features(c)

            def turn_weights(g):
                pe.wait_ge(w_ready, g + 1)
                for h in range(ZG):
                    mm = pe.transpose(banks[T_BANKS[g]][:, h * 128:(h + 1) * 128], w[:, g * ZG + h, :], ident[:])
                mm.then_inc(wT_psum, 1)

            def gather(g):
                pe.wait_ge(wT_ready, g + 1)
                pe.wait_ge(ft_ready, g + 1)
                pe.wait_ge(ft_ones, 1)
                pe.wait_ge(res_ready, g + 1)
                for h in range(ZG):
                    hh = g * ZG + h
                    mm = pe.matmul(banks[1 + g][:, h * (DH1 + 1):(h + 1) * (DH1 + 1)], wT[:, hh, :], ft[:, hh, :],
                                   start=True, stop=True)
                mm.then_inc(gagg_psum, 1)

            keep_warm(5, 8)
            turn_weights(0)
            keep_warm(5, 8)
            turn_weights(1)
            gather(0)
            turn_weights(2)
            gather(1)
            gather(2)

        @block.scalar
        def _(act):
            act.dma_start(bias_sb[:], biases).then_inc(in_bias, 16)
            act.dma_start(small[:], small_in).then_inc(in_small, 16)

            def std_of(n):
                act.wait_ge(stats_ready, n + 1)
                nc.scalar.activation(std[:], mv[:, 1:2], ACT.Sqrt, bias=eps[:]).then_inc(std_ready, 1)

            def turned_relu(n, part, l, out, done):
                for c in range(part * HC, (part + 1) * HC):
                    piece, src = turned(n, c)
                    act.wait_ge(xhatT_psum, piece + 1)
                    if l is None:
                        nc.scalar.activation(out[:, c, :], src, ACT.Relu).then_inc(done, 1)
                    else:
                        nc.scalar.activation(out[:, c, :], src, ACT.Relu, scale=cols[:, l, c:c + 1],
                                             bias=cols[:, L + l, c:c + 1]).then_inc(done, 1)

            def turned_relus(n, l=None):
                turned_relu(n, 0, l, hT_hi, hT_hi_ready)
                turned_relu(n, 0, l, hT, hT_ready)
                turned_relu(n, 1, l, hT, hT_ready)
                act.wait_ge(hT_ready, C * (n + 1))
                nc.scalar.copy(hT_hi[:, HC:C, :], hT[:, HC:C, :]).then_inc(hT_hi_ready, HC)

            def nodesT_high(ver, half):
                act.wait_ge(nodesT_psum, 2 * ver + half + 1)
                nc.scalar.copy(nodesT_hi[:, half * HC:(half + 1) * HC, :],
                               bank3(4 + half, HC)).then_inc(nodesT_hi_ready, 1)

            def agg_high(l, half):
                act.wait_ge(agg_ready, 2 * l + half + 1)
                cs = slice(half * HC, (half + 1) * HC)
                nc.scalar.copy(aggT_hi[:, cs, :], agg[:, cs, :]).then_inc(agg_hi_ready, 1)

            def high(j):
                g, part = j // 2, j % 2
                act.wait_ge(in_slot[g % SLOTS], 16 * (g // SLOTS + 1))
                if j >= JSLOTS:
                    act.wait_ge(job_used, j - JSLOTS + 1)
                nc.scalar.copy(w_hi[:, j % JSLOTS, :, :],
                               ring[:, g % SLOTS, part * JU:(part + 1) * JU, :]).then_inc(hi_ready, 1)

            act.wait_ge(consts, 3)
            nc.scalar.activation(spare[:], eps[:], ACT.Sqrt)
            act.wait_ge(onehot_f, 4)
            std_of(0)
            nc.scalar.copy(oh_dstb[:], oh_dst[:]).then_inc(onehot_b, 1)
            turned_relus(0)
            high(0)
            high(1)
            act.wait_ge(ef_psum, 1)
            for k in range(2):
                ins = nc.scalar.copy(ef_sumT[:, k, :], banks[k][:, 0:128])
            ins.then_inc(ef_ready, 1)
            high(2)
            high(3)
            high(J_N)
            nodesT_high(0, 0)
            high(J_N + 1)
            act.wait_ge(in_small, 16)
            for l in range(L):
                j0 = J_N + J_L * l
                high(j0 + 2)
                nodesT_high(l, 1)
                high(j0 + 3)
                high(j0 + 4)
                agg_high(l, 0)
                agg_high(l, 1)
                for j in range(5, 11):
                    high(j0 + j)
                std_of(1 + l)
                high(j0 + 11)
                turned_relus(1 + l, l)
                high(j0 + 12)
                nodesT_high(1 + l, 0)
                high(j0 + 13)
            high(J_N + J_L * L + 2)
            nodesT_high(L, 1)
            high(J_N + J_L * L + 3)

            def qkv_out(i, dst):
                act.wait_ge(job_used, J_N + J_L * L + QKV_JOB[i] + 1)
                nc.scalar.copy(dst, banks[[0, 1, 2, 3, 0, 1][i]][:, 0:HF]).then_inc(qkv_ready, 1)

            def exps(g):
                act.wait_ge(top_ready, g + 1)
                for h in range(QG):
                    ins = nc.scalar.activation(probs[:, g, h, :], banks[6 + g][:, h * 128:(h + 1) * 128], ACT.Exp,
                                               bias=ntop[:, g, h:h + 1], scale=SCALE,
                                               accum_out=psum_[:, g, h:h + 1])
                ins.then_inc(exp_ready, 1)

            def attn_high(g):
                act.wait_ge(attn_psum, g + 1)
                nc.scalar.copy(attnT_hi[g],
                               banks[2 + g][0:DH0, :].rearrange("p (h n) -> p h n", h=QG)).then_inc(attn_hi_ready, 1)

            def wo_high(k):
                act.wait_ge(in_wo, 16)
                if k < 3:
                    act.wait_ge(job_used, JOBS - 2 + k)
                else:
                    act.wait_ge(wo_used, k - 2)
                nc.scalar.copy(wo_hi[:, k % 3, :, :], wo_chunk(k)).then_inc(wo_hi_ready, 1)

            def probsT_out(g):
                act.wait_ge(probsT_psum, g + 1)
                nc.scalar.copy(probsT[:, g, :, :], bank3(4 + g, QG)).then_inc(probsT_ready, 1)

            j0 = J_N + J_L * L
            high(j0 + 4)
            high(j0 + 5)
            qkv_out(0, qk[:, 0, :])
            qkv_out(1, qk[:, 1, :])
            high(j0 + 6)
            high(j0 + 7)
            qkv_out(2, qk[:, 2, :])
            high(j0 + 8)
            exps(0)
            high(j0 + 9)
            qkv_out(3, qk[:, 3, :])
            high(j0 + 10)
            qkv_out(4, v[:, 0, :])
            high(j0 + 11)
            probsT_out(0)
            wo_high(0)
            exps(1)
            qkv_out(5, v[:, 1, :])
            attn_high(0)
            wo_high(1)
            probsT_out(1)
            wo_high(2)
            attn_high(1)
            wo_high(3)

            std_of(1 + L)
            turned_relu(1 + L, 0, None, hT, hT_ready)
            turned_relu(1 + L, 1, None, hT, hT_ready)
            nc.scalar.activation(spare[:], eps[:], ACT.Exp)

            def features_out(b):
                act.wait_ge(ft_psum, b + 1)
                src = banks[1 + b][:].rearrange("p (c t h o) -> p c t h o", c=2, t=2, h=2)
                nc.scalar.copy(ft[:, 4 * b:4 * b + 4, 0:DH1].rearrange("p (c h) o -> p c h o", c=2),
                               src[:, :, 0, :, :]).then_inc(ft_ready, 1)
                nc.scalar.copy(res[:, 4 * b:4 * b + 4, :].rearrange("p (c h) o -> p c h o", c=2),
                               src[:, :, 1, :, :]).then_inc(res_ready, 1)

            def slopes(g):
                act.wait_ge(z_psum, g + 1)
                nc.scalar.activation(w[:, g * ZG:(g + 1) * ZG, :], bank3(Z_BANKS[g], ZG), ACT.Copy,
                                     scale=SLOPE).then_inc(slope_ready, 1)

            def exp_weights(g):
                act.wait_ge(nzm_ready, g + 1)
                for h in range(g * ZG, (g + 1) * ZG):
                    ins = nc.scalar.activation(w[:, h, :], zl[:, h, :], ACT.Exp, bias=nzm[:, h:h + 1])
                ins.then_inc(w_ready, 1)

            features_out(0)
            for g in range(NG):
                slopes(g)
            exp_weights(0)
            exp_weights(1)
            exp_weights(2)
            features_out(1)
            features_out(2)
            act.wait_ge(rden_ready, 1)
            for h in range(ZG):
                ins = nc.scalar.activation(y[:, h * DH1:(h + 1) * DH1],
                                           banks[1][:, h * (DH1 + 1):h * (DH1 + 1) + DH1], ACT.Copy,
                                           scale=rden[:, h:h + 1])
            ins.then_inc(scaled, 1)

        @block.vector
        def _(dve):
            links = [0]

            def link(ins):
                links[0] += 1
                ins.then_inc(dve_step, 1)
                dve.wait_ge(dve_step, links[0])

            V = nc.vector
            dve.wait_ge(in_idx, 16)
            dve.wait_ge(consts, 3)
            link(V.tensor_copy(idxf[:], idx_sb[:]))
            for j in range(ET):
                ins = V.tensor_scalar(oh_dst[:, j, :], iota[:], idxf[:, 1, j:j + 1], None, ALU.is_equal)
                if j + 1 in EF_LOADS:
                    ins.then_inc(onehot_f, 1)

            dve.wait_ge(in_bias, 16)
            link(V.tensor_copy(bias_p[:, 0, :], bias_sb[:]))
            link(V.tensor_tensor(bias_r[:, 0, :], bias_sb[:], bias_p[:, 0, :], ALU.subtract))
            link(V.tensor_copy(bias_p[:, 1, :], bias_r[:, 0, :]))
            V.tensor_tensor(bias_p[:, 2, :], bias_r[:, 0, :], bias_p[:, 1, :], ALU.subtract).then_inc(bias_split, 1)

            def stats_half(half, src):
                return V.bn_stats(stats[:, half, :], src)

            def aggregate_stats():
                V.bn_aggr(mv[:], stats[:].rearrange("p a b -> p (a b)")).then_inc(stats_ready, 1)

            def normalise(n, halves):
                dve.wait_ge(std_ready, n + 1)
                link(V.reciprocal(rstd[:], std[:]))
                for a, b, _ in PIECES[n]:
                    half, at = a // HC, a % HC * 128
                    V.tensor_scalar(xhat[:, a * 128:b * 128], halves[half][:, at:at + (b - a) * 128],
                                    mv[:, 0:1], rstd[:, 0:1], ALU.subtract, ALU.mult).then_inc(xhat_ready, 1)

            dve.wait_ge(in_x, 16)
            link(stats_half(0, x_sb[:, 0:HF]))
            link(stats_half(1, x_sb[:, HF:D]))
            aggregate_stats()
            normalise(0, [x_sb[:, 0:HF], x_sb[:, HF:D]])
            for j in range(ET):
                ins = V.tensor_scalar(oh_srcb[:, j, :], iota[:], idxf[:, 0, j:j + 1], None, ALU.is_equal)
            ins.then_inc(onehot_b, 1)

            def nodes_out(ver, half):
                hs = slice(half * HF, (half + 1) * HF)
                dve.wait_ge(job_used, nodes_done(ver, half))
                if ver == 0:
                    V.tensor_copy(nodes[:, hs], banks[2 + half][:, 0:HF]).then_inc(nodes_ready, 1)
                else:
                    V.tensor_tensor(nodes[:, hs], banks[2 + half][:, 0:HF], nodes[:, hs],
                                    ALU.add).then_inc(nodes_ready, 1)

            def nodesT_low(ver, half):
                dve.wait_ge(nodesT_hi_ready, 2 * ver + half + 1)
                cs = slice(half * HC, (half + 1) * HC)
                V.tensor_tensor(nodesT_lo[:, cs, :], bank3(4 + half, HC), nodesT_hi[:, cs, :].bitcast(F32),
                                ALU.subtract).then_inc(nodesT_lo_ready, 1)

            def agg_sum(l, half):
                dve.wait_ge(agg_psum, 2 * l + half + 1)
                if l == 0:
                    dve.wait_ge(edge_ready, half + 1)
                cs = slice(half * HC, (half + 1) * HC)
                V.tensor_tensor(agg[:, cs, :], bank3(6 + half, HC), edgeT[:, cs, :], ALU.add).then_inc(agg_ready, 1)

            def low(j):
                g, part = j // 2, j % 2
                dve.wait_ge(hi_ready, j + 1)
                V.tensor_tensor(w_lo[:, j % JSLOTS, :, :], ring[:, g % SLOTS, part * JU:(part + 1) * JU, :],
                                w_hi[:, j % JSLOTS, :, :].bitcast(F32), ALU.subtract).then_inc(lo_ready, 1)

            def hT_low(n, part):
                dve.wait_ge(hT_ready, C * n + (part + 1) * HC)
                dve.wait_ge(hT_hi_ready, C * n + (part + 1) * HC)
                cs = slice(part * HC, (part + 1) * HC)
                V.tensor_tensor(hT_lo[:, cs, :], hT[:, cs, :], hT_hi[:, cs, :].bitcast(F32),
                                ALU.subtract).then_inc(hT_lo_ready, 1)

            dve.wait_ge(count_psum, 1)
            V.tensor_copy(countT[:], banks[6][:, 0:128]).then_inc(count_ready, 1)
            low(0)
            low(1)
            hT_low(0, 0)
            low(2)
            hT_low(0, 1)
            dve.wait_ge(vlr_psum, 1)
            V.tensor_copy(degree[:], banks[7][:, 128:256]).then_inc(count_ready, 1)
            V.tensor_scalar(mask[:], banks[7][:, 0:128], 0.0, MASKED, ALU.is_equal, ALU.mult).then_inc(count_ready, 1)
            dve.wait_ge(wbd_zero, 2)
            for half in range(2):
                rs = slice(half * DH1, (half + 1) * DH1)
                for t in range(2):
                    o = half + NH1 * t
                    V.tensor_copy(vlr[rs, o:o + (C - 1) * 26 + 1:26],
                                  banks[7][rs, 256 + o:256 + o + 11:2]).then_inc(vlr_ready, 1)
            low(3)
            dve.wait_ge(count_ready, 2)
            link(V.tensor_tensor(diag[:], ident[:], degree[:], ALU.mult))
            V.tensor_tensor(mixT[:], diag[:], countT[:], ALU.add).then_inc(mix_ready, 1)

            def edges_out(half):
                dve.wait_ge(edge_psum, half + 1)
                dve.wait_ge(in_small, 16)
                for c in range(half * HC, (half + 1) * HC):
                    ins = V.scalar_tensor_tensor(out=edgeT[:, c, :], in0=degree[:], scalar=cols[:, 2 * L, c:c + 1],
                                                 in1=banks[6 + half][:, c % HC * 128:(c % HC + 1) * 128],
                                                 op0=ALU.mult, op1=ALU.add)
                ins.then_inc(edge_ready, 1)

            nodes_out(0, 0)
            edges_out(0)
            low(J_N)
            nodesT_low(0, 0)
            nodes_out(0, 1)
            edges_out(1)
            low(J_N + 1)
            for l in range(L):
                j0 = J_N + J_L * l
                low(j0 + 2)
                nodesT_low(l, 1)
                agg_sum(l, 0)
                agg_sum(l, 1)
                for j in range(3, 9):
                    low(j0 + j)
                dve.wait_ge(job_used, j0 + J_1 - 2)
                link(stats_half(0, banks[0][:, 0:HF]))
                dve.wait_ge(job_used, j0 + J_1)
                link(stats_half(1, banks[1][:, 0:HF]))
                aggregate_stats()
                normalise(1 + l, [banks[0][:, 0:HF], banks[1][:, 0:HF]])
                low(j0 + 9)
                hT_low(1 + l, 0)
                low(j0 + 10)
                hT_low(1 + l, 1)
                low(j0 + 11)
                nodes_out(1 + l, 0)
                low(j0 + 12)
                nodesT_low(1 + l, 0)
                nodes_out(1 + l, 1)
                low(j0 + 13)

            j0 = J_N + J_L * L
            low(j0 + 2)
            nodesT_low(L, 1)
            low(j0 + 3)
            low(j0 + 4)

            def qkT_out(i):
                dve.wait_ge(qkT_psum, i + 1)
                V.tensor_copy((qT if i % 2 == 0 else kT)[:, i // 2, :, :],
                              banks[4 + i % 2][0:DH0, :].rearrange("p (h n) -> p h n", h=QG)).then_inc(qkT_ready, 1)

            def tops(g):
                dve.wait_ge(score_psum, g + 1)
                link(V.tensor_reduce(top[:, g, :], bank3(6 + g, QG), AX.X, ALU.max))
                V.tensor_scalar(ntop[:, g, :], top[:, g, :], -SCALE, None, ALU.mult).then_inc(top_ready, 1)

            def divide(g):
                dve.wait_ge(exp_ready, g + 1)
                link(V.reciprocal(prec[:, g, :], psum_[:, g, :]))
                V.tensor_tensor(probs[:, g, :, :], probs[:, g, :, :],
                                prec[:, g, :].unsqueeze(2).to_broadcast([128, QG, 128]), ALU.mult).then_inc(probs_ready, 1)

            def attn_low(g):
                dve.wait_ge(attn_hi_ready, g + 1)
                V.tensor_tensor(attnT_lo[g], banks[2 + g][0:DH0, :].rearrange("p (h n) -> p h n", h=QG),
                                attnT_hi[g].bitcast(F32), ALU.subtract).then_inc(attn_lo_ready, 1)

            def wo_low(k):
                dve.wait_ge(wo_hi_ready, k + 1)
                V.tensor_tensor(wo_lo[:, k % 3, :, :], wo_chunk(k), wo_hi[:, k % 3, :, :].bitcast(F32),
                                ALU.subtract).then_inc(wo_lo_ready, 1)

            low(j0 + 5)
            qkT_out(0)
            qkT_out(1)
            low(j0 + 6)
            low(j0 + 7)
            tops(0)
            low(j0 + 8)
            low(j0 + 9)
            qkT_out(2)
            qkT_out(3)
            divide(0)
            low(j0 + 10)
            low(j0 + 11)
            tops(1)
            wo_low(0)
            divide(1)
            attn_low(0)
            wo_low(1)
            wo_low(2)
            attn_low(1)
            wo_low(3)

            for half in range(2):
                hs = slice(half * HF, (half + 1) * HF)
                dve.wait_ge(wo_used, 3 + half)
                link(stats_half(half, banks[6 + half][:, 0:HF]))
            aggregate_stats()
            normalise(1 + L, [banks[6][:, 0:HF], banks[7][:, 0:HF]])
            for half in range(2):
                V.tensor_copy(x1[:, half * HF:(half + 1) * HF], banks[6 + half][:, 0:HF]).then_inc(x1_ready, 1)
            R = 2 * NH1
            dve.wait_ge(a_psum, 1)
            dve.wait_ge(a_parts_zero, 1)
            a_bank = banks[0][0:R, 0:128]
            link(V.tensor_copy(a_parts[0:R, :], a_bank))
            link(V.tensor_tensor(a_rest[:], a_bank, a_parts[0:R, :], ALU.subtract))
            V.tensor_copy(a_parts[32:32 + R, :], a_rest[:])
            link(V.tensor_copy(a_mid[:], a_rest[:]))
            V.tensor_tensor(a_parts[64:64 + R, :], a_rest[:], a_mid[:], ALU.subtract).then_inc(a_ready, 1)

            def leaky(g):
                hs = slice(g * ZG, (g + 1) * ZG)
                dve.wait_ge(slope_ready, g + 1)
                link(V.tensor_tensor(zl[:, hs, :], bank3(Z_BANKS[g], ZG), w[:, hs, :], ALU.max))
                V.tensor_reduce(nzm[:, hs], zl[:, hs, :], AX.X, ALU.max, negate=True).then_inc(nzm_ready, 1)

            def weigh(g):
                hs = slice(g * ZG, (g + 1) * ZG)
                dve.wait_ge(wT_psum, g + 1)
                V.tensor_tensor(wT[:, hs, :], bank3(T_BANKS[g], ZG),
                                countT[:].unsqueeze(1).to_broadcast([128, ZG, 128]), ALU.mult).then_inc(wT_ready, 1)

            def sums_of(g):
                return banks[1 + g][:, 0:ZG * (DH1 + 1)].rearrange("p (h o) -> p h o", h=ZG)

            def weight_sums(g):
                dve.wait_ge(gagg_psum, g + 1)
                hs = slice(g * ZG, (g + 1) * ZG)
                return V.tensor_scalar(den[:, hs], sums_of(g)[:, :, DH1], 1e-16, None, ALU.max)

            def reciprocals(g):
                hs = slice(g * ZG, (g + 1) * ZG)
                return V.reciprocal(rden[:, hs], den[:, hs])

            def scaled_plus_residual(g):
                for h in range(ZG):
                    hh = g * ZG + h
                    ins = V.scalar_tensor_tensor(out=y[:, hh * DH1:(hh + 1) * DH1], in0=sums_of(g)[:, h, 0:DH1],
                                                 scalar=rden[:, hh:hh + 1], in1=res[:, hh, :],
                                                 op0=ALU.mult, op1=ALU.add)
                return ins

            def result(g):
                cs = slice(g * ZG * DH1, (g + 1) * ZG * DH1)
                V.scalar_tensor_tensor(out=y[:, cs], in0=y[:, cs], scalar=0.0,
                                       in1=x1[:, cs], op0=ALU.max, op1=ALU.add).then_inc(y_ready, 1)

            leaky(0)
            leaky(1)
            leaky(2)
            weigh(0)
            weigh(1)
            link(weight_sums(0))
            reciprocals(0).then_inc(rden_ready, 1)
            weigh(2)
            link(weight_sums(1))
            link(reciprocals(1))
            dve.wait_ge(res_ready, NG)
            scaled_plus_residual(1).then_inc(dve_step, 1)
            weight_sums(2).then_inc(dve_step, 1)
            dve.wait_ge(dve_step, links[0] + 1)
            result(1)
            dve.wait_ge(dve_step, links[0] + 2)
            links[0] += 2
            link(reciprocals(2))
            link(scaled_plus_residual(2))
            result(2)


def kernel(**inputs):
    import numpy as np
    import concourse.bacc as bacc
    from concourse.bass_utils import run_bass_kernel_spmd as run

    a = {k: np.asarray(v) for k, v in inputs.items()}

    def units(w):
        o, i = w.shape
        return w.T.reshape(i // 128, 128, o // HF, HF).transpose(2, 0, 1, 3)

    pre = "L0_gnn_"
    quarters = lambda u: [u[0, 0:HC], u[1, 0:HC], u[0, HC:C], u[1, HC:C]]
    stream = quarters(units(a[pre + "Wn"]))
    for l in range(L):
        u = units(a[pre + "W1"][l])
        stream += quarters(u) + [u[0, C:], u[1, C:]]
        stream += quarters(units(a[pre + "W2"][l]))
    q0, q1, k0, k1, v0, v1 = units(a[pre + "Wqkv"])
    stream += [q0[0:HC], k0[0:HC], q0[HC:C], k0[HC:C], q1, k1, v0, v1]
    stream = np.concatenate(stream)
    twice = lambda m: np.concatenate([m, m])
    arrays = {
        "x": a["x"],
        "idx": np.stack([a["src"].reshape(128, ET), a["dst"].reshape(128, ET)], 1),
        "ef": a["edge_attr_256"].reshape(128, ET, DE),
        "wstream": stream.reshape(GROUPS, GU, 128, HF).transpose(0, 2, 1, 3),
        "we": a[pre + "We"].T.reshape(DE // 128, 128, D).transpose(1, 0, 2),
        "wo": a[pre + "Wo"].T.reshape(NH0, DH0, D).transpose(1, 0, 2),
        "biases": np.concatenate([a[pre + n].reshape(-1) for n in ("b1", "bn", "b2", "bo", "bqkv")]).reshape(BR, 128),
        "small_in": np.concatenate([
            np.concatenate([a[pre + n].reshape(-1, C, 128) for n in ("ln_g", "ln_b", "be")]).transpose(2, 0, 1)
            .reshape(128, -1),
            twice(a["L1_gnn_W"]), twice(a["L1_gnn_W"]),
            twice(a["L1_gnn_attn_l"][0].T), twice(a["L1_gnn_attn_r"][0].T),
            twice(a["L1_gnn_W"].T), twice(a["L1_gnn_W_res"].T)], 1),
    }
    arrays = {k: np.ascontiguousarray(v) for k, v in arrays.items()}
    nc = bacc.Bacc("TRN2", target_bir_lowering=False, num_devices=1)
    args = [nc.dram_tensor(k, v.shape, mybir.dt.from_np(v.dtype), kind="ExternalInput").ap() for k, v in arrays.items()]
    out = nc.dram_tensor("out", (N, D), F32, kind="ExternalOutput").ap()
    build(nc, *args, out)
    r = run(nc, [arrays], core_ids=[0])
    return r.results[0]["out"]
```
